# Optimizing a Trainium2 kernel written in Bass

```python
import numpy as np
import jax
import jax.numpy as jnp

def _softmax(x, axis=-1):
    return jax.nn.softmax(x, axis=axis)

def _gelu(x):
    return jax.nn.gelu(x, approximate=True)

def _silu(x):
    return jax.nn.silu(x)

def _sigmoid(x):
    return jax.nn.sigmoid(x)

def _layernorm(x, axis=-1, eps=1e-05):
    m = jnp.mean(x, axis=axis, keepdims=True)
    v = jnp.var(x, axis=axis, keepdims=True)
    return (x - m) / jnp.sqrt(v + eps)

def _scatter_add(tgt, idx, src, axis=0):
    return tgt.at[idx].add(src)

def _segment_sum(src, seg, n):
    return jax.ops.segment_sum(src, seg, n)
kernel_name = 'mk_macaron_d1_jaxref_r8_c0410f'

def setup_inputs(seed: int=0):
    np.random.seed(seed)
    _w = jnp.asarray

    def _L0_attn_setup():
        import jax, jax.numpy as jnp
        import numpy as np
        DIM = 128
        N_HEADS = 16
        HEAD_DIM = DIM // N_HEADS
        HIDDEN = 352
        WINDOW_PER_SIDE = 128
        EPS = 1e-05
        THETA = 10000.0

        def rope_cos_sin(seqlen, head_dim):
            freqs = 1.0 / THETA ** (jnp.arange(0, head_dim, 2, dtype=jnp.float32) / head_dim)
            t = jnp.arange(seqlen, dtype=jnp.float32)
            ang = jnp.outer(t, freqs)
            return (jnp.cos(ang), jnp.sin(ang))

        def apply_rope(x, cos, sin):
            xr = x[..., 0::2]
            xi = x[..., 1::2]
            c = cos[None, :, None, :]
            s = sin[None, :, None, :]
            or_ = xr * c - xi * s
            oi_ = xr * s + xi * c
            return jnp.stack([or_, oi_], axis=-1).reshape(x.shape)

        def layernorm(x, g, b):
            mu = jnp.mean(x, axis=-1, keepdims=True)
            var = jnp.mean(jnp.square(x - mu), axis=-1, keepdims=True)
            return (x - mu) * jax.lax.rsqrt(var + EPS) * g + b

        def attention(x, wq, wk, wv, wo):
            b, s, _ = x.shape
            scale = HEAD_DIM ** (-0.5)
            q = (x @ wq).reshape(b, s, N_HEADS, HEAD_DIM)
            k = (x @ wk).reshape(b, s, N_HEADS, HEAD_DIM)
            v = (x @ wv).reshape(b, s, N_HEADS, HEAD_DIM)
            cos, sin = rope_cos_sin(s, HEAD_DIM)
            q = apply_rope(q, cos, sin)
            k = apply_rope(k, cos, sin)
            i = jnp.arange(s)[:, None]
            j = jnp.arange(s)[None, :]
            mask = (j <= i) & (i - j <= WINDOW_PER_SIDE)
            scores = jnp.einsum('bqhd,bkhd->bhqk', q, k) * scale
            scores = jnp.where(mask[None, None], scores, jnp.finfo(scores.dtype).min)
            probs = jax.nn.softmax(scores, axis=-1)
            out = jnp.einsum('bhqk,bkhd->bqhd', probs, v).reshape(b, s, -1)
            return out @ wo

        def ffn(x, w1, w2, w3):
            return jax.nn.silu(x @ w1) * (x @ w3) @ w2
        key = jax.random.key(seed)
        ks = jax.random.split(key, 9)
        sd = 0.02
        x = jax.random.normal(ks[0], (4, 256, DIM), dtype=jnp.float32)
        wq = jax.random.normal(ks[1], (DIM, DIM), dtype=jnp.float32) * sd
        wk = jax.random.normal(ks[2], (DIM, DIM), dtype=jnp.float32) * sd
        wv = jax.random.normal(ks[3], (DIM, DIM), dtype=jnp.float32) * sd
        wo = jax.random.normal(ks[4], (DIM, DIM), dtype=jnp.float32) * sd
        w1 = jax.random.normal(ks[5], (DIM, HIDDEN), dtype=jnp.float32) * sd
        w2 = jax.random.normal(ks[6], (HIDDEN, DIM), dtype=jnp.float32) * sd
        w3 = jax.random.normal(ks[7], (DIM, HIDDEN), dtype=jnp.float32) * sd
        ln1_g = jnp.ones((DIM,), jnp.float32)
        ln1_b = jnp.zeros((DIM,), jnp.float32)
        ln2_g = jnp.ones((DIM,), jnp.float32)
        ln2_b = jnp.zeros((DIM,), jnp.float32)
        return dict(x=x, wq=wq, wk=wk, wv=wv, wo=wo, w1=w1, w2=w2, w3=w3, ln1_g=ln1_g, ln1_b=ln1_b, ln2_g=ln2_g, ln2_b=ln2_b)
    _L0_attn_in = _L0_attn_setup()

    def _L0_ffn_setup():
        import jax, jax.numpy as jnp
        import numpy as np
        INPUT_SIZE = 128
        OUTPUT_SIZE = 128
        key = jax.random.key(seed)
        kx, kt, kp, ktn, kpn = jax.random.split(key, 5)
        x = jax.random.normal(kx, (8, 256, INPUT_SIZE), dtype=jnp.float32)
        theta = jax.random.normal(kt, (INPUT_SIZE, OUTPUT_SIZE), dtype=jnp.float32) * 0.02
        phi = jax.random.normal(kp, (INPUT_SIZE, OUTPUT_SIZE), dtype=jnp.float32) * 0.02
        theta_noise = jax.random.normal(ktn, (INPUT_SIZE, OUTPUT_SIZE), dtype=jnp.float32) * 0.01
        phi_noise = jax.random.normal(kpn, (INPUT_SIZE, OUTPUT_SIZE), dtype=jnp.float32) * 0.01
        return {'x': x, 'theta': theta, 'phi': phi, 'theta_noise': theta_noise, 'phi_noise': phi_noise}
    _L0_ffn_in = _L0_ffn_setup()
    _d = {'L0_attn_x': _L0_attn_in['x'], 'L0_attn_wq': _L0_attn_in['wq'], 'L0_attn_wk': _L0_attn_in['wk'], 'L0_attn_wv': _L0_attn_in['wv'], 'L0_attn_wo': _L0_attn_in['wo'], 'L0_attn_w1': _L0_attn_in['w1'], 'L0_attn_w2': _L0_attn_in['w2'], 'L0_attn_w3': _L0_attn_in['w3'], 'L0_attn_ln1_g': _L0_attn_in['ln1_g'], 'L0_attn_ln1_b': _L0_attn_in['ln1_b'], 'L0_attn_ln2_g': _L0_attn_in['ln2_g'], 'L0_attn_ln2_b': _L0_attn_in['ln2_b'], 'L0_ffn_theta': _L0_ffn_in['theta'], 'L0_ffn_phi': _L0_ffn_in['phi'], 'L0_ffn_theta_noise': _L0_ffn_in['theta_noise'], 'L0_ffn_phi_noise': _L0_ffn_in['phi_noise']}
    _x0 = _d['L0_attn_x']
    _d['L0_attn_x'] = jax.random.normal(jax.random.fold_in(jax.random.key(seed), 1), (8, 512, 128), dtype=_x0.dtype)
    del _x0
    return _d

def reference(L0_attn_x, L0_attn_wq, L0_attn_wk, L0_attn_wv, L0_attn_wo, L0_attn_w1, L0_attn_w2, L0_attn_w3, L0_attn_ln1_g, L0_attn_ln1_b, L0_attn_ln2_g, L0_attn_ln2_b, L0_ffn_theta, L0_ffn_phi, L0_ffn_theta_noise, L0_ffn_phi_noise):

    def _L0_attn_ref(x, wq, wk, wv, wo, w1, w2, w3, ln1_g, ln1_b, ln2_g, ln2_b):
        import jax, jax.numpy as jnp
        import numpy as np
        DIM = 128
        N_HEADS = 16
        HEAD_DIM = DIM // N_HEADS
        HIDDEN = 352
        WINDOW_PER_SIDE = 128
        EPS = 1e-05
        THETA = 10000.0

        def rope_cos_sin(seqlen, head_dim):
            freqs = 1.0 / THETA ** (jnp.arange(0, head_dim, 2, dtype=jnp.float32) / head_dim)
            t = jnp.arange(seqlen, dtype=jnp.float32)
            ang = jnp.outer(t, freqs)
            return (jnp.cos(ang), jnp.sin(ang))

        def apply_rope(x, cos, sin):
            xr = x[..., 0::2]
            xi = x[..., 1::2]
            c = cos[None, :, None, :]
            s = sin[None, :, None, :]
            or_ = xr * c - xi * s
            oi_ = xr * s + xi * c
            return jnp.stack([or_, oi_], axis=-1).reshape(x.shape)

        def layernorm(x, g, b):
            mu = jnp.mean(x, axis=-1, keepdims=True)
            var = jnp.mean(jnp.square(x - mu), axis=-1, keepdims=True)
            return (x - mu) * jax.lax.rsqrt(var + EPS) * g + b

        def attention(x, wq, wk, wv, wo):
            b, s, _ = x.shape
            scale = HEAD_DIM ** (-0.5)
            q = (x @ wq).reshape(b, s, N_HEADS, HEAD_DIM)
            k = (x @ wk).reshape(b, s, N_HEADS, HEAD_DIM)
            v = (x @ wv).reshape(b, s, N_HEADS, HEAD_DIM)
            cos, sin = rope_cos_sin(s, HEAD_DIM)
            q = apply_rope(q, cos, sin)
            k = apply_rope(k, cos, sin)
            i = jnp.arange(s)[:, None]
            j = jnp.arange(s)[None, :]
            mask = (j <= i) & (i - j <= WINDOW_PER_SIDE)
            scores = jnp.einsum('bqhd,bkhd->bhqk', q, k) * scale
            scores = jnp.where(mask[None, None], scores, jnp.finfo(scores.dtype).min)
            probs = jax.nn.softmax(scores, axis=-1)
            out = jnp.einsum('bhqk,bkhd->bqhd', probs, v).reshape(b, s, -1)
            return out @ wo

        def ffn(x, w1, w2, w3):
            return jax.nn.silu(x @ w1) * (x @ w3) @ w2
        h = x + attention(layernorm(x, ln1_g, ln1_b), wq, wk, wv, wo)
        out = h + ffn(layernorm(h, ln2_g, ln2_b), w1, w2, w3)
        return out

    def _L0_ffn_ref(x, theta, phi, theta_noise, phi_noise):
        import jax, jax.numpy as jnp
        import numpy as np
        INPUT_SIZE = 128
        OUTPUT_SIZE = 128
        real = jnp.einsum('bti,io->bto', x, jnp.cos(theta + theta_noise))
        imag = jnp.einsum('bti,io->bto', x, jnp.sin(phi + phi_noise))
        return jnp.sqrt(real * real + imag * imag)
    x = L0_attn_x
    x = x + 0.5 * _L0_ffn_ref(_layernorm(x, axis=-1), L0_ffn_theta, L0_ffn_phi, L0_ffn_theta_noise, L0_ffn_phi_noise)
    x = x + _L0_attn_ref(_layernorm(x, axis=-1), L0_attn_wq, L0_attn_wk, L0_attn_wv, L0_attn_wo, L0_attn_w1, L0_attn_w2, L0_attn_w3, L0_attn_ln1_g, L0_attn_ln1_b, L0_attn_ln2_g, L0_attn_ln2_b)
    x = x + 0.5 * _L0_ffn_ref(_layernorm(x, axis=-1), L0_ffn_theta, L0_ffn_phi, L0_ffn_theta_noise, L0_ffn_phi_noise)
    return x

_drawn_inputs = setup_inputs


def setup_inputs(seed=0):
    import zlib

    import numpy as np

    out = dict(_drawn_inputs(seed))
    spreads = {'L0_attn_ln1_g': (1.0, 0.6),
     'L0_attn_ln1_b': (0.0, 0.8),
     'L0_attn_ln2_g': (1.0, 0.6),
     'L0_attn_ln2_b': (0.0, 0.8)}
    factors = {'L0_attn_wq': 8.0,
     'L0_attn_wk': 8.0,
     'L0_attn_wv': 8.0,
     'L0_attn_wo': 8.0,
     'L0_attn_w1': 8.0,
     'L0_attn_w2': 8.0,
     'L0_attn_w3': 8.0,
     'L0_ffn_theta': 8.0,
     'L0_ffn_theta_noise': 8.0}
    for name, (base, spread) in spreads.items():
        noise = np.random.default_rng([zlib.crc32(name.encode()), seed]).standard_normal(out[name].shape)
        drawn = base * np.exp(spread * noise) if base else spread * noise
        out[name] = jnp.asarray(drawn.astype(out[name].dtype))
    for name, factor in factors.items():
        out[name] = (out[name] * factor).astype(out[name].dtype)
    return out
```

```python
import math

import concourse.bass as bass
import concourse.mybir as mybir
import numpy as np
from contextlib import ExitStack

FP32 = mybir.dt.float32
BF16 = mybir.dt.bfloat16
ALU = mybir.AluOpType
ACT = mybir.ActivationFunctionType
AX = mybir.AxisListType.X

BATCH, SEQ, DIM = 8, 512, 128
HEADS = 16
HD = DIM // HEADS
HIDDEN = 352
P = 128
TILES = SEQ // P
PAIRS = HEADS // 2
QUADS = HEADS // 4
CHUNKS = [(0, 128), (128, 128), (256, 96)]
EPS = 1e-5
TINY = 1e-19
THETA = 10000.0
SCALE = HD ** -0.5
NEG = -1e30
SLOTS_Q = (0, 0, 0, 1, 1, 2)
SLOTS_K = (0, 1, 2, 0, 1, 0)
SPLIT_ROWS = 16 * len(SLOTS_Q)
SHIFT_ROWS = SPLIT_ROWS + 1
K_DMAS, Q_DMAS = 16 * 3, 16 * 12
A_USES = 7
MAX_AT = ((0, 1), (2,), (3,), (4,), (5,), (6,), (), ())
UNITS = 2 * 4 * QUADS


def build(nc, x, cos_t, sin_t, wq, wk, wv, wo, w1, w2, w3, g1, b1, g2, b2,
          theta, phi, theta_n, phi_n, out):
    ctx = ExitStack()
    with ctx:
        def sb(name, shape, dt=FP32):
            return ctx.enter_context(nc.sbuf_tensor(name, shape, dt))

        def sem(name):
            return ctx.enter_context(nc.semaphore(name))

        ident = sb("ident", [P, P])
        ident_b = sb("ident_b", [P, P], BF16)
        band_mask = sb("band_mask", [P, 2, 2 * P], BF16)
        causal_mask = sb("causal_mask", [P, 4, P], BF16)
        cos_sb = sb("cos_sb", [P, SEQ])
        sin_sb = sb("sin_sb", [P, SEQ])
        wqk = sb("wqk", [P, 4, P])
        wv_sb = sb("wv_sb", [P, P])
        wo_sb = sb("wo_sb", [P, P])
        w1_sb = sb("w1_sb", [P, HIDDEN])
        w3_sb = sb("w3_sb", [P, HIDDEN])
        w2_sb = sb("w2_sb", [P, 3, P])
        gb = sb("gb", [P, 4])
        raw = sb("raw", [P, 4, P])
        ang = sb("ang", [P, 2, P])
        turns = sb("turns", [P, 2, P])
        spec_w = sb("spec_w", [P, 2 * P])

        xt = sb("xt", [P, 2, TILES, P])
        f_st = sb("f_st", [P, 2, TILES, 6])
        f_mv = sb("f_mv", [P, 2, TILES, 2])
        f_negm = sb("f_negm", [P, 2, TILES])
        f_ln = sb("f_ln", [P, 3, TILES])
        f_rs = sb("f_rs", [P, 4, TILES])
        f_vyt = sb("f_vyt", [P, 2, TILES])
        eps_ap = sb("eps_ap", [P, 4])
        n0 = sb("n0", [P, TILES, P])
        n0T = sb("n0T", [P, SEQ])
        f_sq = sb("f_sq", [P, TILES, 2 * P])
        f_z = sb("f_z", [P, TILES, P])
        x1 = sb("x1", [P, 2, TILES, P])
        y = sb("y", [P, 2, TILES, P])
        yn = sb("yn", [P, TILES, P])
        n1T = sb("n1T", [P, SEQ])
        rot = sb("rot", [P, 2, 2, SEQ])
        roped = sb("roped", [P, 2, SEQ])
        resid = sb("resid", [P, 2, SEQ])
        parts = sb("parts", [P, 2, 3, SEQ], BF16)
        vaug = sb("vaug", [P, 2, TILES, HEADS, 32])
        qz = sb("qz", [P, 2, PAIRS, 2, SEQ], BF16)
        ks = sb("ks", [P, 2, PAIRS, SEQ], BF16)

        mx = sb("mx", [P, 2, 2, 2, TILES])
        mxT = sb("mxT", [16, 2, P], BF16)
        prob = sb("prob", [P, 4, 2, 2, 2 * P])
        o_sb = sb("o_sb", [P, SEQ])
        rden = sb("rden", [P, TILES, 4])
        attn = sb("attn", [P, TILES, P])

        t_st = sb("t_st", [P, 2, TILES, 6])
        t_mv = sb("t_mv", [P, 2, TILES, 2])
        t_negm = sb("t_negm", [P, 2, TILES])
        t_ln = sb("t_ln", [P, 2, TILES])
        t_rs = sb("t_rs", [P, 2, TILES])
        attnT = sb("attnT", [P, SEQ])
        h = sb("h", [P, TILES, P])
        hx1 = sb("hx1", [P, TILES, P])
        n2 = sb("n2", [P, TILES, P])
        n2T = sb("n2T", [P, SEQ])
        up = sb("up", [P, 3, SEQ])
        sg = sb("sg", [P, 5, SEQ])
        act_up = sb("act_up", [P, 3, SEQ])
        gated = sb("gated", [P, 3, SEQ])
        x2 = sb("x2", [P, TILES, P])
        n3 = sb("n3", [P, TILES, P])
        n3T = sb("n3T", [P, SEQ])
        t_sq = sb("t_sq", [P, TILES, 2 * P])
        t_z = sb("t_z", [P, TILES, P])
        x3 = sb("x3", [P, TILES, P])

        s_ps = ctx.enter_context(nc.psum_tensor("s_ps", [P, 3, 512], FP32))
        a_ps = ctx.enter_context(nc.psum_tensor("a_ps", [P, 2, 512], FP32))
        o_ps = ctx.enter_context(nc.psum_tensor("o_ps", [P, 512], FP32))
        f_ps = ctx.enter_context(nc.psum_tensor("f_ps", [P, 512], FP32))
        t_ps = ctx.enter_context(nc.psum_tensor("t_ps", [P, 512], FP32))

        weights_in = sem("weights_in")
        consts_made = sem("consts_made")
        masks_made = sem("masks_made")
        consts_dve = sem("consts_dve")
        angles = sem("angles")
        angle_step = sem("angle_step")
        spec_ready = sem("spec_ready")
        rot_ready = sem("rot_ready")
        x_in = sem("x_in")
        x_stats = sem("x_stats")
        x_mv = sem("x_mv")
        x_negm = sem("x_negm")
        x_lnvar = sem("x_lnvar")
        x_rstd = sem("x_rstd")
        n0_ready = sem("n0_ready")
        front_mm = sem("front_mm")
        front_act = sem("front_act")
        front_dve = sem("front_dve")
        z1_ready = sem("z1_ready")
        lnz1 = sem("lnz1")
        mag1 = sem("mag1")
        x1_ready = sem("x1_ready")
        x1_stats = sem("x1_stats")
        x1_mv = sem("x1_mv")
        x1_negm = sem("x1_negm")
        x1_lnvar = sem("x1_lnvar")
        x1_rstd = sem("x1_rstd")
        vy_part = sem("vy_part")
        vy_ready = sem("vy_ready")
        vy_ln = sem("vy_ln")
        vy_rstd = sem("vy_rstd")
        rs2_ready = sem("rs2_ready")
        y_ready = sem("y_ready")
        yn_ready = sem("yn_ready")
        roped_ready = sem("roped_ready")
        high_ready = sem("high_ready")
        resid_q = sem("resid_q")
        resid_k = sem("resid_k")
        mid_ready = sem("mid_ready")
        low_q = sem("low_q")
        low_k = sem("low_k")
        q_spilled = sem("q_spilled")
        k_spilled = sem("k_spilled")
        k_stacked = sem("k_stacked")
        q_stacked = sem("q_stacked")
        max_scores = sem("max_scores")
        max_done = sem("max_done")
        maxT_mm = sem("maxT_mm")
        maxT_out = sem("maxT_out")
        shift_in = sem("shift_in")
        scores = sem("scores")
        exp_done = sem("exp_done")
        masked = sem("masked")
        pv_done = sem("pv_done")
        o_out = sem("o_out")
        oT_mm = sem("oT_mm")
        den_done = sem("den_done")
        attn_done = sem("attn_done")
        tail_mm = sem("tail_mm")
        tail_dve = sem("tail_dve")
        tail_act = sem("tail_act")
        h_stats = sem("h_stats")
        h_mv = sem("h_mv")
        h_negm = sem("h_negm")
        h_lnvar = sem("h_lnvar")
        h_rstd = sem("h_rstd")
        n2_ready = sem("n2_ready")
        hx1_ready = sem("hx1_ready")
        silu_e = sem("silu_e")
        silu_l = sem("silu_l")
        silu_s = sem("silu_s")
        silu_u = sem("silu_u")
        x2_stats = sem("x2_stats")
        x2_mv = sem("x2_mv")
        x2_negm = sem("x2_negm")
        x2_lnvar = sem("x2_lnvar")
        x2_rstd = sem("x2_rstd")
        n3_ready = sem("n3_ready")
        z2_ready = sem("z2_ready")
        lnz2 = sem("lnz2")
        mag2 = sem("mag2")
        x3_ready = sem("x3_ready")
        stored = sem("stored")
        waits_passed = sem("waits_passed")

        q_dram = nc.dram_tensor("q_dram", (3, P, SEQ), BF16).ap()
        k_dram = nc.dram_tensor("k_dram", (PAIRS, 3, 16, SEQ), BF16).ap()

        block = ctx.enter_context(nc.Block())
        N_WEIGHTS = 18
        last = BATCH - 1

        def wait_alone(eng, s, n):
            eng.wait_ge(s, n)
            eng.sem_inc(waits_passed, 1)

        def batches(eng, front, body, tail):
            front(0, 0)
            body(0, 0, True, False)
            with eng.Fori(0, (BATCH - 2) // 2) as pair:
                body(2 * pair + 1, 1, True, True)
                body(2 * pair + 2, 0, True, True)
            body(last, last % 2, False, True)
            tail(last, last % 2)

        @block.sync
        def _(sp):
            for dst, src in (
                (raw[:, 0, :], theta), (raw[:, 1, :], theta_n), (raw[:, 2, :], phi), (raw[:, 3, :], phi_n),
                (wqk[:, 0, :], wq), (wqk[:, 2, :], wk), (wv_sb[:, :], wv), (cos_sb[:, :], cos_t),
                (sin_sb[:, :], sin_t), (wo_sb[:, :], wo), (w1_sb[:, :], w1), (w3_sb[:, :], w3),
                (w2_sb[:, 0:2, :], w2[0:256, :].rearrange("(c p) d -> p c d", p=P)),
                (w2_sb[0:96, 2, :], w2[256:352, :]),
                (gb[:, 0:1], g1), (gb[:, 1:2], b1), (gb[:, 2:3], g2), (gb[:, 3:4], b2),
            ):
                sp.dma_start(dst, src).then_inc(weights_in, 16)

            sp.sem_inc(stored, 16)

            def load_x(f, p):
                if not (isinstance(f, int) and f < 2):
                    wait_alone(sp, x1_ready, f - 1)
                sp.dma_start(xt[:, p, :, :], x[f].rearrange("(t p) d -> p t d", p=P)).then_inc(x_in, 16)

            def stack(f, p):
                if not (isinstance(f, int) and f < 1):
                    wait_alone(sp, q_stacked, Q_DMAS * f)
                    wait_alone(sp, k_stacked, K_DMAS * f)
                def spill_q(part, s, n):
                    sp.wait_ge(s, n)
                    sp.dma_start(q_dram[part], parts[:, 0, part, :]).then_inc(q_spilled, 16)

                def spill_k(part, s, n):
                    sp.wait_ge(s, n)
                    sp.dma_start(k_dram[:, part], parts[:, 1, part, :]).then_inc(k_spilled, 16)

                def stack_q(part):
                    wait_alone(sp, q_spilled, 48 * f + 16 * (part + 1))
                    if part == 0 and not (isinstance(f, int) and f < 2):
                        sp.wait_ge(pv_done, 16 * (f - 1))
                    src = q_dram[part].rearrange("(s g d) n -> g d s n", g=2, d=HD)
                    for j in range(len(SLOTS_Q)):
                        for g in range(2) if SLOTS_Q[j] == part else ():
                            sp.dma_start(qz[16 * j + 8 * g:16 * j + 8 * g + 8, p, :, g, :], src[g]).then_inc(q_stacked, 16)

                def stack_k(row, n):
                    sp.wait_ge(k_spilled, 48 * f + 16 * n)
                    sp.dma_start(ks[row:row + 16 * n, p, :, :],
                                 k_dram[:, 0:n].rearrange("s a r n -> (a r) s n")).then_inc(k_stacked, 16)

                spill_q(0, high_ready, 2 * f + 1)
                stack_q(0)
                spill_k(0, high_ready, 2 * f + 2)
                spill_q(1, mid_ready, 2 * f + 1)
                stack_q(1)
                stack_k(80, 1)
                spill_q(2, low_q, f + 1)
                spill_k(1, mid_ready, 2 * f + 2)
                stack_q(2)
                stack_k(48, 2)
                spill_k(2, low_k, f + 1)
                stack_k(0, 3)

            def store(w):
                wait_alone(sp, x3_ready, w + 1)
                sp.dma_start(out[w].rearrange("(t p) d -> p t d", p=P), x3[:, :, :]).then_inc(stored, 16)

            def step(f, p):
                stack(f, p)
                if not (isinstance(f, int) and f == last):
                    load_x(f + 1, 1 - p)
                if not (isinstance(f, int) and f < 2):
                    store(f - 2)

            load_x(0, 0)
            step(0, 0)
            step(1, 1)
            with sp.Fori(1, BATCH // 2 - 1) as pair:
                step(2 * pair, 0)
                step(2 * pair + 1, 1)
            step(BATCH - 2, 0)
            step(last, 1)
            store(BATCH - 2)
            store(last)
            sp.wait_ge(stored, 16 * BATCH + 16)

        @block.gpsimd
        def _(pool):
            for n, (t, v) in enumerate(((ident, 0.0), (ident_b, 0.0), (band_mask, 0.0), (causal_mask, 0.0))):
                nc.gpsimd.memset(t[:], v).then_inc(consts_made, 1)
            pool.wait_ge(consts_made, 4)
            nc.gpsimd.memset(ks[96:128, :, :, :], 1.0).then_inc(masks_made, 1)
            pool.wait_ge(masks_made, 1)
            for t in (ident, ident_b):
                nc.gpsimd.affine_select(out=t[:, :], in_=t[:, :], compare_op=ALU.not_equal, fill=1.0, base=0,
                                        pattern=[[-1, P]], channel_multiplier=1).then_inc(masks_made, 1)
            nc.gpsimd.affine_select(out=causal_mask[:], in_=causal_mask[:], compare_op=ALU.is_ge, fill=NEG, base=0,
                                    pattern=[[0, 4], [-1, P]], channel_multiplier=1).then_inc(masks_made, 1)
            nc.gpsimd.affine_select(out=band_mask[:], in_=band_mask[:], compare_op=ALU.is_ge, fill=NEG, base=0,
                                    pattern=[[0, 2], [1, 2 * P]], channel_multiplier=-1).then_inc(consts_made, 1)
            pool.wait_ge(consts_made, 5)
            nc.gpsimd.affine_select(out=band_mask[:], in_=band_mask[:], compare_op=ALU.is_ge, fill=NEG, base=P,
                                    pattern=[[0, 2], [-1, 2 * P]], channel_multiplier=1).then_inc(masks_made, 1)

            def norm(dst, src, negm, rs, done):
                for t in range(TILES):
                    ins = nc.gpsimd.tensor_scalar(dst[:, t, :], src[:, t, :], negm[:, t:t + 1], rs[:, t:t + 1],
                                                  ALU.add, ALU.mult)
                ins.then_inc(done, 1)

            def f_n0(f, p):
                pool.wait_ge(x_rstd, f + 1)
                wait_alone(pool, x_negm, f + 1)
                norm(n0, xt[:, p], f_negm[:, 0], f_rs[:, 0], n0_ready)

            def f_yn(f, p):
                pool.wait_ge(rs2_ready, f + 1)
                wait_alone(pool, x1_negm, f + 1)
                norm(yn, x1[:, p], f_negm[:, 1], f_rs[:, 3], yn_ready)

            def f_rope(f, i):
                pool.wait_ge(front_dve, 6 * f + 3 + 2 * i)
                nc.gpsimd.tensor_tensor(roped[:, i, :], rot[:, i, 0, :], rot[:, i, 1, :], ALU.add).then_inc(roped_ready, 1)

            def f_resid_q(f):
                pool.wait_ge(high_ready, 2 * f + 1)
                nc.gpsimd.tensor_tensor(resid[:, 0, :], roped[:, 0, :], parts[:, 0, 0, :], ALU.subtract).then_inc(resid_q, 1)

            def f_low_q(f):
                pool.wait_ge(mid_ready, 2 * f + 1)
                pool.wait_ge(resid_q, f + 1)
                nc.gpsimd.tensor_tensor(parts[:, 0, 2, :], resid[:, 0, :], parts[:, 0, 1, :], ALU.subtract).then_inc(low_q, 1)

            def mask(b, s):
                kt = s % 4
                wait_alone(pool, exp_done, 32 * b + 2 * s + 2)
                own = prob[:, s % 4, :, :, 0:P].rearrange("p a g n -> p (a g) n")
                ins = nc.gpsimd.affine_select(out=own, in_=own, compare_op=ALU.is_ge, fill=0.0, base=0,
                                              pattern=[[0, 4], [1, P]], channel_multiplier=-1)
                if kt < 3:
                    nxt = prob[:, s % 4, :, :, P:2 * P].rearrange("p a g n -> p (a g) n")
                    ins = nc.gpsimd.affine_select(out=nxt, in_=nxt, compare_op=ALU.is_ge, fill=0.0, base=0,
                                                  pattern=[[0, 4], [-1, P]], channel_multiplier=1)
                ins.then_inc(masked, 1)

            def t_n2(w):
                pool.wait_ge(h_rstd, w + 1)
                wait_alone(pool, h_negm, w + 1)
                norm(n2, h, t_negm[:, 0], t_rs[:, 0], n2_ready)

            def t_u(w, c):
                pool.wait_ge(silu_s, 3 * w + c + 1)
                r = CHUNKS[c][1]
                nc.gpsimd.tensor_tensor(act_up[0:r, c, :], up[0:r, c, :], sg[0:r, 2 + c, :], ALU.mult).then_inc(silu_u, 1)

            def t_n3(w):
                pool.wait_ge(x2_rstd, w + 1)
                wait_alone(pool, x2_negm, w + 1)
                norm(n3, x2, t_negm[:, 1], t_rs[:, 1], n3_ready)

            def first(f, p):
                f_n0(f, p)
                f_yn(f, p)
                f_rope(f, 0)
                f_resid_q(f)
                f_low_q(f)
                f_rope(f, 1)

            def body(b, p, has_front, has_tail):
                f, w = b + 1, b - 1
                for h in range(UNITS):
                    if h % 2 == 1:
                        mask(b, h // 2)
                    if has_front:
                        if h == 1:
                            f_n0(f, 1 - p)
                        if h == 11:
                            f_yn(f, 1 - p)
                        if h == 15:
                            f_rope(f, 0)
                        if h == 17:
                            f_resid_q(f)
                            f_rope(f, 1)
                        if h == 19:
                            f_low_q(f)
                    if has_tail:
                        if h == 9:
                            t_n2(w)
                        if h in (14, 16, 18):
                            t_u(w, (h - 14) // 2)
                        if h == 25:
                            t_n3(w)

            def tail(w, p):
                t_n2(w)
                for c in range(3):
                    t_u(w, c)
                t_n3(w)

            batches(pool, first, body, tail)

        @block.scalar
        def _(act):
            act.sem_inc(tail_act, 3)
            act.wait_ge(angles, 6)
            nc.scalar.activation(spec_w[:, 0:P], ang[:, 0, :], ACT.Sin).then_inc(spec_ready, 1)
            nc.scalar.activation(spec_w[:, P:2 * P], ang[:, 1, :], ACT.Sin).then_inc(spec_ready, 1)

            act.preload_act_table_set("natural_log_exp_and_others")

            def rsqrt(dst, tmp, var, lnsem, done, n):
                nc.scalar.activation(tmp, var, ACT.Ln, bias=eps_ap[:, 0:1]).then_inc(lnsem, 1)
                act.wait_ge(lnsem, n)
                nc.scalar.activation(dst, tmp, ACT.Exp, scale=-0.5).then_inc(done, 1)

            def magnitude(dst, tmp, z, lnsem, done, n):
                nc.scalar.activation(tmp, z, ACT.Ln, bias=eps_ap[:, 1:2]).then_inc(lnsem, 1)
                act.wait_ge(lnsem, n)
                nc.scalar.activation(dst, tmp, ACT.Exp, scale=0.5, bias=eps_ap[:, 2:3]).then_inc(done, 1)

            def f_rs0(f):
                act.wait_ge(x_mv, f + 1)
                rsqrt(f_rs[:, 0, :], f_ln[:, 0, :], f_mv[:, 0, :, 1], x_lnvar, x_rstd, f + 1)

            def f_n0T(f):
                act.wait_ge(front_mm, 9 * f + 1)
                nc.scalar.activation(n0T[:, :], f_ps[:, :], ACT.Copy).then_inc(front_act, 1)

            def f_square(f, half):
                act.wait_ge(front_mm, 9 * f + 2 + half)
                nc.scalar.activation(f_sq[:, 2 * half:2 * half + 2, :].rearrange("p t n -> p (t n)"), f_ps[:, :],
                                     ACT.Square).then_inc(front_act, 1)

            def f_mag1(f):
                act.wait_ge(z1_ready, f + 1)
                magnitude(f_z[:, :, :], f_z[:, :, :], f_z[:, :, :], lnz1, mag1, f + 1)

            def f_rs1(f):
                act.wait_ge(x1_mv, f + 1)
                rsqrt(f_rs[:, 1, :], f_ln[:, 1, :], f_mv[:, 1, :, 1], x1_lnvar, x1_rstd, f + 1)

            def f_rs2(f):
                act.wait_ge(vy_ready, f + 1)
                rsqrt(f_rs[:, 2, :], f_ln[:, 2, :], f_vyt[:, 1, :], vy_ln, vy_rstd, f + 1)

            def f_high(f, i):
                act.wait_ge(roped_ready, 2 * f + i + 1)
                if not (isinstance(f, int) and f < 1):
                    act.wait_ge(k_spilled if i else q_spilled, 48 * f)
                nc.scalar.activation(parts[:, i, 0, :], roped[:, i, :], ACT.Copy).then_inc(high_ready, 1)

            def f_mid(f, i):
                act.wait_ge(resid_k if i else resid_q, f + 1)
                nc.scalar.activation(parts[:, i, 1, :], resid[:, i, :], ACT.Copy).then_inc(mid_ready, 1)

            def maxT(a, c):
                act.wait_ge(maxT_mm, 4 * a + c + 1)
                if not (isinstance(a, int) and 4 * a + c < 2):
                    act.wait_ge(shift_in, 16 * (4 * a + c - 1))
                nc.scalar.activation(mxT[:, c % 2, :], a_ps[0:16, 1, 0:P], ACT.Copy, scale=-1.0).then_inc(maxT_out, 1)

            def shift(a, p, c):
                act.wait_ge(maxT_out, 4 * a + c + 1)
                dst = qz[SPLIT_ROWS:SHIFT_ROWS, p, 2 * c:2 * c + 2, :, :].rearrange("o s g n -> o (s g n)")
                act.dma_start(dst, mxT[:, c % 2, :]).then_inc(shift_in, 16)

            def exp(b, v):
                kt = (v % 8) // 2
                act.wait_ge(scores, 32 * b + v + 1)
                if not (isinstance(b, int) and 16 * b + v // 2 < 4):
                    act.wait_ge(pv_done, 16 * b + v // 2 - 3)
                n = 2 * P if kt < 3 else P
                bank = s_ps[:, v % 3, 0:2 * n].rearrange("p (g n) -> p g n", g=2)
                nc.scalar.activation(prob[:, (v // 2) % 4, v % 2, :, 0:n], bank, ACT.Exp, scale=SCALE).then_inc(exp_done, 1)

            def o_copy(b, c):
                act.wait_ge(pv_done, 16 * b + 4 * c + 4)
                nc.scalar.activation(o_sb[:, :], o_ps[:, :], ACT.Copy).then_inc(o_out, 1)

            def t_rs0(w):
                act.wait_ge(h_mv, w + 1)
                rsqrt(t_rs[:, 0, :], t_ln[:, 0, :], t_mv[:, 0, :, 1], h_lnvar, h_rstd, w + 1)

            def t_sig(w, c):
                r = CHUNKS[c][1]
                act.wait_ge(tail_dve, 10 * w + 4 + c)
                nc.scalar.activation(sg[0:r, 0, :], up[0:r, c, :], ACT.Exp, scale=-1.0).then_inc(silu_e, 1)
                act.wait_ge(silu_e, 3 * w + c + 1)
                nc.scalar.activation(sg[0:r, 1, :], sg[0:r, 0, :], ACT.Ln, bias=eps_ap[0:r, 3:4]).then_inc(silu_l, 1)
                act.wait_ge(silu_l, 3 * w + c + 1)
                nc.scalar.activation(sg[0:r, 2 + c, :], sg[0:r, 1, :], ACT.Exp, scale=-1.0).then_inc(silu_s, 1)

            def t_rs1(w):
                act.wait_ge(x2_mv, w + 1)
                rsqrt(t_rs[:, 1, :], t_ln[:, 1, :], t_mv[:, 1, :, 1], x2_lnvar, x2_rstd, w + 1)

            def t_n3T(w):
                act.wait_ge(tail_mm, 13 * w + 11)
                nc.scalar.activation(n3T[:, :], t_ps[:, :], ACT.Copy).then_inc(tail_act, 1)

            def t_square(w, half):
                act.wait_ge(tail_mm, 13 * w + 12 + half)
                nc.scalar.activation(t_sq[:, 2 * half:2 * half + 2, :].rearrange("p t n -> p (t n)"), t_ps[:, :],
                                     ACT.Square).then_inc(tail_act, 1)

            def t_mag2(w):
                act.wait_ge(z2_ready, w + 1)
                magnitude(t_z[:, :, :], t_z[:, :, :], t_z[:, :, :], lnz2, mag2, w + 1)

            def first(f, p):
                f_rs0(f)
                f_n0T(f)
                f_square(f, 0)
                f_square(f, 1)
                f_mag1(f)
                f_rs1(f)
                f_rs2(f)
                f_high(f, 0)
                f_mid(f, 0)
                f_high(f, 1)
                f_mid(f, 1)
                maxT(f, 0)
                shift(f, p, 0)

            def body(b, p, has_front, has_tail):
                f, w = b + 1, b - 1
                for h in range(UNITS):
                    exp(b, h)
                    if h == 2 and has_tail:
                        o_copy(w, 3)
                    if h in (10, 18, 26):
                        o_copy(b, h // 8 - 1)
                    if h in (6, 14, 22):
                        maxT(b, h // 8 + 1)
                        shift(b, p, h // 8 + 1)
                    if h == 30 and has_front:
                        maxT(f, 0)
                        shift(f, 1 - p, 0)
                    if has_tail:
                        if h == 8:
                            t_rs0(w)
                        if h in (13, 15, 17):
                            t_sig(w, (h - 13) // 2)
                        if h == 24:
                            t_rs1(w)
                        if h == 26:
                            t_n3T(w)
                        if h in (27, 28):
                            t_square(w, h - 27)
                        if h == 30:
                            t_mag2(w)
                    if has_front:
                        if h == 0:
                            f_rs0(f)
                        if h == 3:
                            f_n0T(f)
                        if h in (4, 5):
                            f_square(f, h - 4)
                        if h == 7:
                            f_mag1(f)
                        if h == 9:
                            f_rs1(f)
                        if h == 10:
                            f_rs2(f)
                        if h == 16:
                            f_high(f, 0)
                        if h == 18:
                            f_high(f, 1)
                            f_mid(f, 0)
                        if h == 20:
                            f_mid(f, 1)

            def tail(w, p):
                o_copy(w, 3)
                t_rs0(w)
                for c in range(3):
                    t_sig(w, c)
                t_rs1(w)
                t_n3T(w)
                t_square(w, 0)
                t_square(w, 1)
                t_mag2(w)

            batches(act, first, body, tail)

        @block.vector
        def _(dve):
            nc.vector.memset(qz[:], 0.0).then_inc(consts_dve, 1)
            nc.vector.memset(vaug[:], 1.0).then_inc(consts_dve, 1)
            for i, v in enumerate((EPS, TINY, math.log(0.5), 1.0)):
                nc.vector.memset(eps_ap[:, i:i + 1], v).then_inc(consts_dve, 1)
            dve.wait_ge(weights_in, 16 * N_WEIGHTS)
            nc.vector.tensor_tensor(ang[:, 0, :], raw[:, 0, :], raw[:, 1, :], ALU.add).then_inc(angles, 1)
            nc.vector.tensor_tensor(ang[:, 1, :], raw[:, 2, :], raw[:, 3, :], ALU.add).then_inc(angles, 1)
            dve.wait_ge(angles, 2)
            nc.vector.tensor_scalar(ang[:, 0, :], ang[:, 0, :], math.pi / 2, None, ALU.add).then_inc(angle_step, 1)
            dve.wait_ge(angle_step, 1)
            big = 1.5 * 2 ** 23
            nc.vector.tensor_scalar(turns[:], ang[:], 1 / (2 * math.pi), big, ALU.mult, ALU.add).then_inc(angle_step, 1)
            dve.wait_ge(angle_step, 2)
            nc.vector.tensor_scalar(turns[:], turns[:], big, None, ALU.subtract).then_inc(angle_step, 1)
            dve.wait_ge(angle_step, 3)
            nc.vector.scalar_tensor_tensor(out=ang[:], in0=turns[:], scalar=-6.28125, in1=ang[:],
                                           op0=ALU.mult, op1=ALU.add).then_inc(angle_step, 1)
            dve.wait_ge(angle_step, 4)
            nc.vector.scalar_tensor_tensor(out=ang[:], in0=turns[:], scalar=-(2 * math.pi - 6.28125), in1=ang[:],
                                           op0=ALU.mult, op1=ALU.add).then_inc(angle_step, 1)
            dve.wait_ge(angle_step, 5)
            nc.vector.tensor_scalar(ang[:], ang[:], float(np.float32(3.1415925)), -float(np.float32(3.1415925)),
                                    ALU.min, ALU.max).then_inc(angles, 4)
            for i in (0, 2):
                src = wqk[:, i, :].rearrange("p (j e) -> p j e", e=2)
                dst = wqk[:, i + 1, :].rearrange("p (j e) -> p j e", e=2)
                nc.vector.tensor_scalar(dst[:, :, 0], src[:, :, 1], -1.0, None, ALU.mult).then_inc(rot_ready, 1)
                nc.vector.tensor_copy(dst[:, :, 1], src[:, :, 0]).then_inc(rot_ready, 1)

            def stats(src, st, mv, negm, s_st, s_mv, s_neg, n):
                for t in range(TILES):
                    ins = nc.vector.bn_stats(st[:, t, :], src[:, t, :])
                ins.then_inc(s_st, 1)
                wait_alone(dve, s_st, n)
                for t in range(TILES):
                    ins = nc.vector.bn_aggr(mv[:, t, :], st[:, t, :])
                ins.then_inc(s_mv, 1)
                dve.wait_ge(s_mv, n)
                nc.vector.tensor_scalar(negm, mv[:, :, 0], -1.0, None, ALU.mult).then_inc(s_neg, 1)

            def f_stats0(f, p):
                dve.wait_ge(x_in, 16 * (f + 1))
                stats(xt[:, p], f_st[:, 0], f_mv[:, 0], f_negm[:, 0, :], x_stats, x_mv, x_negm, f + 1)

            def f_x1(f, p):
                dve.wait_ge(front_act, 3 * f + 3)
                nc.vector.tensor_tensor(f_z[:, :, :], f_sq[:, :, 0:P], f_sq[:, :, P:2 * P], ALU.add).then_inc(z1_ready, 1)

            def f_x1b(f, p):
                dve.wait_ge(mag1, f + 1)
                nc.vector.tensor_tensor(x1[:, p, :, :], xt[:, p, :, :], f_z[:, :, :], ALU.add).then_inc(x1_ready, 1)
                dve.wait_ge(x1_ready, f + 1)
                stats(x1[:, p], f_st[:, 1], f_mv[:, 1], f_negm[:, 1, :], x1_stats, x1_mv, x1_negm, f + 1)

            def f_vy(f):
                dve.wait_ge(x1_rstd, f + 1)
                nc.vector.tensor_tensor(f_vyt[:, 0, :], f_mv[:, 1, :, 1], f_rs[:, 1, :], ALU.mult).then_inc(vy_part, 1)
                dve.wait_ge(vy_part, f + 1)
                nc.vector.tensor_tensor(f_vyt[:, 1, :], f_vyt[:, 0, :], f_rs[:, 1, :], ALU.mult).then_inc(vy_ready, 1)

            def f_y(f, p):
                for t in range(TILES):
                    ins = nc.vector.tensor_scalar(y[:, p, t, :], x1[:, p, t, :], f_negm[:, 1, t:t + 1],
                                                  f_rs[:, 1, t:t + 1], ALU.add, ALU.mult)
                ins.then_inc(y_ready, 1)

            def f_rs2(f):
                dve.wait_ge(vy_rstd, f + 1)
                nc.vector.tensor_tensor(f_rs[:, 3, :], f_rs[:, 1, :], f_rs[:, 2, :], ALU.mult).then_inc(rs2_ready, 1)

            def f_n1T(f):
                dve.wait_ge(front_mm, 9 * f + 4)
                nc.vector.tensor_scalar(n1T[:, :], f_ps[:, :], gb[:, 0:1], gb[:, 1:2], ALU.mult, ALU.add).then_inc(front_dve, 1)

            def f_rot(f, i, j):
                dve.wait_ge(front_mm, 9 * f + 5 + 2 * i + j)
                nc.vector.tensor_tensor(rot[:, i, j, :], f_ps[:, :], (sin_sb if j else cos_sb)[:, :], ALU.mult).then_inc(front_dve, 1)

            def f_v(f, p):
                dve.wait_ge(front_mm, 9 * f + 9)
                if not (isinstance(f, int) and f < 2):
                    dve.wait_ge(pv_done, 16 * (f - 1))
                nc.vector.tensor_copy(vaug[:, p, :, :, 0:HD].rearrange("p t h d -> p (t h) d"),
                                      f_ps[:, :].rearrange("p (a d) -> p a d", d=HD)).then_inc(front_dve, 1)

            def f_resid_k(f):
                dve.wait_ge(high_ready, 2 * f + 2)
                nc.vector.tensor_tensor(resid[:, 1, :], roped[:, 1, :], parts[:, 1, 0, :], ALU.subtract).then_inc(resid_k, 1)

            def f_low_k(f):
                dve.wait_ge(mid_ready, 2 * f + 2)
                nc.vector.tensor_tensor(parts[:, 1, 2, :], resid[:, 1, :], parts[:, 1, 1, :], ALU.subtract).then_inc(low_k, 1)

            def amax(a, c, j):
                dve.wait_ge(max_scores, A_USES * (4 * a + c) + j + 1)
                bank = a_ps[:, j % 2, :]
                if j == 0:
                    dst = mx[:, c % 2, :, :, 0]
                    src = bank.rearrange("p (s g n) -> p s g n", s=2, g=2)
                else:
                    t, pr = (j + 1) // 2, (j + 1) % 2
                    dst, src = mx[:, c % 2, pr, :, t], bank.rearrange("p (g n) -> p g n", g=2)
                nc.vector.tensor_reduce(dst, src, AX, ALU.max).then_inc(max_done, 1)

            def o_norm(b, c):
                dve.wait_ge(oT_mm, 4 * b + c + 1)
                oT = o_ps[:, :].rearrange("p (t h n) -> p t h n", t=TILES, h=4)
                nc.vector.reciprocal(rden[:, :, :], oT[:, :, :, HD]).then_inc(den_done, 1)
                dve.wait_ge(den_done, 4 * b + c + 1)
                if c == 0 and not (isinstance(b, int) and b < 1):
                    dve.wait_ge(tail_mm, 13 * (b - 1) + 1)
                for t in range(TILES):
                    dst = attn[:, t, 32 * c:32 * c + 32].rearrange("p (h d) -> p h d", h=4)
                    ins = nc.vector.tensor_tensor(dst, oT[:, t, :, 0:HD],
                                                  rden[:, t, :].unsqueeze(2).to_broadcast([P, 4, HD]), ALU.mult)
                ins.then_inc(attn_done, 1)

            def t_attnT(w):
                dve.wait_ge(tail_mm, 13 * w + 1)
                nc.vector.tensor_copy(attnT[:, :], t_ps[:, :]).then_inc(tail_dve, 1)

            def t_h(w, p):
                dve.wait_ge(tail_mm, 13 * w + 2)
                nc.vector.tensor_tensor(h[:, :, :], t_ps[:, :].rearrange("p (t n) -> p t n", t=TILES),
                                        y[:, p, :, :], ALU.add).then_inc(tail_dve, 1)
                dve.wait_ge(tail_dve, 10 * w + 2)
                nc.vector.tensor_tensor(hx1[:, :, :], h[:, :, :], x1[:, p, :, :], ALU.add).then_inc(hx1_ready, 1)
                stats(h, t_st[:, 0], t_mv[:, 0], t_negm[:, 0, :], h_stats, h_mv, h_negm, w + 1)

            def t_n2T(w):
                dve.wait_ge(tail_mm, 13 * w + 3)
                nc.vector.tensor_scalar(n2T[:, :], t_ps[:, :], gb[:, 2:3], gb[:, 3:4], ALU.mult, ALU.add).then_inc(tail_dve, 1)

            def t_up(w, c):
                r = CHUNKS[c][1]
                dve.wait_ge(tail_mm, 13 * w + 4 + c)
                nc.vector.tensor_scalar(up[0:r, c, :], t_ps[0:r, :], -43.0, None, ALU.max).then_inc(tail_dve, 1)

            def t_gate(w, c):
                r = CHUNKS[c][1]
                dve.wait_ge(tail_mm, 13 * w + 7 + c)
                dve.wait_ge(silu_u, 3 * w + c + 1)
                nc.vector.tensor_tensor(gated[0:r, c, :], t_ps[0:r, :], act_up[0:r, c, :], ALU.mult).then_inc(tail_dve, 1)

            def t_x2(w):
                dve.wait_ge(tail_mm, 13 * w + 10)
                dve.wait_ge(hx1_ready, w + 1)
                nc.vector.tensor_tensor(x2[:, :, :], t_ps[:, :].rearrange("p (t n) -> p t n", t=TILES),
                                        hx1[:, :, :], ALU.add).then_inc(tail_dve, 1)
                dve.wait_ge(tail_dve, 10 * w + 10)
                stats(x2, t_st[:, 1], t_mv[:, 1], t_negm[:, 1, :], x2_stats, x2_mv, x2_negm, w + 1)

            def t_z2(w):
                dve.wait_ge(tail_act, 3 * w + 6)
                nc.vector.tensor_tensor(t_z[:, :, :], t_sq[:, :, 0:P], t_sq[:, :, P:2 * P], ALU.add).then_inc(z2_ready, 1)

            def t_x3(w):
                dve.wait_ge(mag2, w + 1)
                dve.wait_ge(stored, 16 * w + 16)
                nc.vector.tensor_tensor(x3[:, :, :], x2[:, :, :], t_z[:, :, :], ALU.add).then_inc(x3_ready, 1)

            def first(f, p):
                f_stats0(f, p)
                f_x1(f, p)
                f_x1b(f, p)
                f_vy(f)
                f_y(f, p)
                f_rs2(f)
                f_n1T(f)
                f_rot(f, 0, 0)
                f_rot(f, 0, 1)
                f_rot(f, 1, 0)
                f_rot(f, 1, 1)
                f_v(f, p)
                f_resid_k(f)
                f_low_k(f)
                for j in range(A_USES):
                    amax(f, 0, j)

            def body(b, p, has_front, has_tail):
                f, w = b + 1, b - 1
                for h in range(UNITS):
                    c, k = divmod(h, 8)
                    if h == 0 and has_front:
                        f_stats0(f, 1 - p)
                    if c < 3 or has_front:
                        for j in MAX_AT[k]:
                            amax(*((b, c + 1) if c < 3 else (f, 0)), j)
                    if h == 3 and has_tail:
                        o_norm(w, 3)
                    if h in (11, 19, 27):
                        o_norm(b, h // 8 - 1)
                    if has_tail:
                        if h == 4:
                            t_attnT(w)
                        if h == 6:
                            t_h(w, 1 - p)
                        if h == 11:
                            t_n2T(w)
                        if h in (12, 13, 14):
                            t_up(w, h - 12)
                        if h in (15, 17, 19):
                            t_gate(w, (h - 15) // 2)
                        if h == 22:
                            t_x2(w)
                        if h == 29:
                            t_z2(w)
                        if h == 31:
                            t_x3(w)
                    if has_front:
                        if h == 6:
                            f_x1(f, 1 - p)
                        if h == 8:
                            f_x1b(f, 1 - p)
                        if h == 9:
                            f_vy(f)
                            f_y(f, 1 - p)
                        if h == 10:
                            f_rs2(f)
                        if h == 12:
                            f_n1T(f)
                        if h in (13, 14, 15, 16):
                            f_rot(f, (h - 13) // 2, (h - 13) % 2)
                        if h == 17:
                            f_v(f, 1 - p)
                        if h == 19:
                            f_resid_k(f)
                        if h == 21:
                            f_low_k(f)

            def tail(w, p):
                o_norm(w, 3)
                t_attnT(w)
                t_h(w, p)
                t_n2T(w)
                for c in range(3):
                    t_up(w, c)
                for c in range(3):
                    t_gate(w, c)
                t_x2(w)
                t_z2(w)
                t_x3(w)

            batches(dve, first, body, tail)

        @block.tensor
        def _(pe):
            mm = nc.tensor.matmul
            pe.wait_ge(masks_made, 5)
            pe.wait_ge(consts_dve, 6)
            pe.wait_ge(weights_in, 16 * N_WEIGHTS)
            pe.wait_ge(rot_ready, 4)
            pe.wait_ge(spec_ready, 2)

            def transposes(dst, src, done):
                for t in range(TILES):
                    ins = nc.tensor.transpose(dst[:, t * P:(t + 1) * P], src[:, t, :], ident[:, :])
                ins.then_inc(done, 1)

            def spectral(dst, srcT, half, done):
                for i in range(2):
                    t = 2 * half + i
                    ins = mm(dst[:, i * 2 * P:(i + 1) * 2 * P], srcT[:, t * P:(t + 1) * P], spec_w[:, :],
                             start=True, stop=True)
                ins.then_inc(done, 1)

            def f_T0(f):
                pe.wait_ge(n0_ready, f + 1)
                if not (isinstance(f, int) and f < 1):
                    pe.wait_ge(front_dve, 6 * f)
                transposes(f_ps, n0, front_mm)

            def f_spec(f, half):
                pe.wait_ge(front_act, 3 * f + 1 + half)
                spectral(f_ps, n0T, half, front_mm)

            def f_T1(f):
                pe.wait_ge(yn_ready, f + 1)
                pe.wait_ge(front_act, 3 * f + 3)
                transposes(f_ps, yn, front_mm)

            def f_proj(f, i):
                pe.wait_ge(front_dve, 6 * f + 1 + i)
                mm(f_ps[:, :], wqk[:, i, :], n1T[:, :], start=True, stop=True).then_inc(front_mm, 1)

            def f_v(f):
                pe.wait_ge(front_dve, 6 * f + 5)
                for t in range(TILES):
                    ins = mm(f_ps[:, t * P:(t + 1) * P], n1T[:, t * P:(t + 1) * P], wv_sb[:, :], start=True, stop=True)
                ins.then_inc(front_mm, 1)

            def amax(a, p, c, j):
                quad = 4 * a + c
                if c == 0 and j == 0:
                    pe.wait_ge(k_stacked, K_DMAS * (a + 1))
                    pe.wait_ge(q_stacked, Q_DMAS * (a + 1))
                first_ever = isinstance(a, int) and a == 0 and c == 0
                if j >= 2 or (j == 0 and not first_ever):
                    pe.wait_ge(max_done, A_USES * quad + max(j - 1, 0))
                if j == 1 and not first_ever:
                    pe.wait_ge(maxT_out, quad)
                bank = a_ps[:, j % 2, :]
                if j == 0:
                    mm(bank, ident_b[:, :], causal_mask[:].rearrange("p h n -> p (h n)"), start=True, stop=True)
                    for hh in range(4):
                        pr, g = 2 * c + hh // 2, hh % 2
                        ins = mm(bank[:, hh * P:(hh + 1) * P], qz[0:SPLIT_ROWS, p, pr, g, 0:P],
                                 ks[0:SPLIT_ROWS, p, pr, 0:P], start=False, stop=True, skip_group_check=True)
                else:
                    t, pr = (j + 1) // 2, 2 * c + (j + 1) % 2
                    mm(bank, ident_b[:, :], band_mask[:].rearrange("p h n -> p (h n)"), start=True, stop=True)
                    for g in range(2):
                        ins = mm(bank[:, g * 2 * P:(g + 1) * 2 * P], qz[0:SPLIT_ROWS, p, pr, g, t * P:(t + 1) * P],
                                 ks[0:SPLIT_ROWS, p, pr, (t - 1) * P:(t + 1) * P], start=False, stop=True,
                                 skip_group_check=True)
                ins.then_inc(max_scores, 1)

            def maxT(a, c):
                pe.wait_ge(max_done, A_USES * (4 * a + c + 1))
                nc.tensor.transpose(a_ps[0:16, 1, 0:P], mx[:, c % 2, :, :, :].rearrange("p s g t -> p (s g t)"),
                                    ident[:, :]).then_inc(maxT_mm, 1)

            def score(b, p, v):
                c, kt, pr = v // 8, (v % 8) // 2, 2 * (v // 8) + v % 2
                if v % 8 == 0:
                    pe.wait_ge(shift_in, 16 * (4 * b + c + 1))
                if not (isinstance(b, int) and 32 * b + v < 3):
                    pe.wait_ge(exp_done, 32 * b + (v - 2 if v > 1 else v - 1))
                n = 2 * P if kt < 3 else P
                mm(s_ps[:, v % 3, 0:2 * n], ks[0:SHIFT_ROWS, p, pr, kt * P:(kt + 1) * P],
                   qz[0:SHIFT_ROWS, p, pr, :, kt * P:kt * P + n], start=True, stop=True).then_inc(scores, 1)

            def pv(b, p, s):
                c, kt = divmod(s, 4)
                pe.wait_ge(masked, 16 * b + s + 1)
                if kt == 0 and not (isinstance(b, int) and 4 * b + c < 1):
                    pe.wait_ge(attn_done, 4 * b + c)
                n = 2 * P if kt < 3 else P
                for hh in range(4):
                    ins = mm(o_ps[32 * hh:32 * hh + 32, kt * P:kt * P + n], vaug[:, p, kt, 4 * c + hh, :],
                             prob[:, s % 4, hh // 2, hh % 2, 0:n], start=(kt == 0), stop=(kt == 3),
                             skip_group_check=True)
                ins.then_inc(pv_done, 1)

            def oT(b, c):
                pe.wait_ge(o_out, 4 * b + c + 1)
                for t in range(TILES):
                    ins = nc.tensor.transpose(o_ps[:, t * P:(t + 1) * P], o_sb[:, t * P:(t + 1) * P], ident[:, :])
                ins.then_inc(oT_mm, 1)

            def t_attn(w):
                pe.wait_ge(attn_done, 4 * w + 4)
                pe.wait_ge(tail_act, 3 * w + 3)
                transposes(t_ps, attn, tail_mm)

            def t_wo(w):
                pe.wait_ge(tail_dve, 10 * w + 1)
                for t in range(TILES):
                    ins = mm(t_ps[:, t * P:(t + 1) * P], attnT[:, t * P:(t + 1) * P], wo_sb[:, :], start=True, stop=True)
                ins.then_inc(tail_mm, 1)

            def t_n2(w):
                pe.wait_ge(n2_ready, w + 1)
                pe.wait_ge(tail_dve, 10 * w + 2)
                transposes(t_ps, n2, tail_mm)

            def t_ffn(w, i):
                at, r = CHUNKS[i % 3]
                pe.wait_ge(tail_dve, 10 * w + 3 + i)
                mm(t_ps[0:r, :], (w3_sb if i >= 3 else w1_sb)[:, at:at + r], n2T[:, :], start=True, stop=True).then_inc(tail_mm, 1)

            def t_w2(w, half):
                if half == 0:
                    pe.wait_ge(tail_dve, 10 * w + 9)
                for t in (2 * half, 2 * half + 1):
                    for c, (_, r) in enumerate(CHUNKS):
                        ins = mm(t_ps[:, t * P:(t + 1) * P], gated[0:r, c, t * P:(t + 1) * P], w2_sb[0:r, c, :],
                                 start=(c == 0), stop=(c == 2))
                if half == 1:
                    ins.then_inc(tail_mm, 1)

            def t_n3(w):
                pe.wait_ge(n3_ready, w + 1)
                pe.wait_ge(tail_dve, 10 * w + 10)
                transposes(t_ps, n3, tail_mm)

            def t_spec(w, half):
                pe.wait_ge(tail_act, 3 * w + 4 + half)
                spectral(t_ps, n3T, half, tail_mm)

            def first(f, p):
                f_T0(f)
                f_spec(f, 0)
                f_spec(f, 1)
                f_T1(f)
                for i in range(4):
                    f_proj(f, i)
                f_v(f)
                for j in range(A_USES):
                    amax(f, p, 0, j)
                maxT(f, 0)

            def body(b, p, has_front, has_tail):
                f, w = b + 1, b - 1
                for h in range(UNITS):
                    c, k = divmod(h, 8)
                    uses = MAX_AT[k] if c < 3 or has_front else ()
                    a = (b, p, c + 1) if c < 3 else (f, 1 - p, 0)
                    score(b, p, h)
                    if k == 6 and (c < 3 or has_front):
                        maxT(a[0], a[2])
                    for j in uses[0:1]:
                        amax(*a, j)
                    if h == 3 and has_tail:
                        oT(w, 3)
                    if h in (11, 19, 27):
                        oT(b, h // 8 - 1)
                    if has_tail:
                        if h == 11:
                            t_n2(w)
                        if h in (12, 13, 14):
                            t_ffn(w, h - 12)
                        if h in (15, 17, 19):
                            t_ffn(w, 3 + (h - 15) // 2)
                        if h in (20, 21):
                            t_w2(w, h - 20)
                        if h == 26:
                            t_n3(w)
                        if h in (27, 28):
                            t_spec(w, h - 27)
                    for j in uses[1:]:
                        amax(*a, j)
                    if has_tail:
                        if h == 4:
                            t_attn(w)
                        if h == 5:
                            t_wo(w)
                    if has_front:
                        if h == 3:
                            f_T0(f)
                        if h in (4, 5):
                            f_spec(f, h - 4)
                        if h == 12:
                            f_T1(f)
                        if h in (13, 14, 15, 16):
                            f_proj(f, h - 13)
                        if h == 17:
                            f_v(f)
                    if h == 1 and has_tail:
                        pv(w, 1 - p, 15)
                    if h % 2 == 1 and h >= 5:
                        s = (h - 3) // 2
                        if s % 4 == 1:
                            pv(b, p, s - 1)
                        if s % 4 != 0:
                            pv(b, p, s)

            def tail(w, p):
                pv(w, p, 15)
                oT(w, 3)
                t_attn(w)
                t_wo(w)
                t_n2(w)
                for i in range(6):
                    t_ffn(w, i)
                t_w2(w, 0)
                t_w2(w, 1)
                t_n3(w)
                t_spec(w, 0)
                t_spec(w, 1)

            batches(pe, first, body, tail)


_INS = ['L0_attn_x', 'L0_attn_wq', 'L0_attn_wk', 'L0_attn_wv', 'L0_attn_wo', 'L0_attn_w1', 'L0_attn_w2', 'L0_attn_w3',
        'L0_attn_ln1_g', 'L0_attn_ln1_b', 'L0_attn_ln2_g', 'L0_attn_ln2_b', 'L0_ffn_theta', 'L0_ffn_phi',
        'L0_ffn_theta_noise', 'L0_ffn_phi_noise']


def rope_tables():
    freqs = (1.0 / np.float32(THETA) ** (np.arange(0, HD, 2, dtype=np.float32) / np.float32(HD))).astype(np.float32)
    angle = np.outer(freqs, np.arange(SEQ, dtype=np.float32)).astype(np.float32)
    rows = np.tile(np.repeat(angle, 2, axis=0), (HEADS, 1))
    return np.cos(rows).astype(np.float32), np.sin(rows).astype(np.float32)


def kernel(**inputs):
    import concourse.bacc as bacc
    from concourse.bass_utils import run_bass_kernel_spmd as run

    nc = bacc.Bacc("TRN2", target_bir_lowering=False, num_devices=1)
    arrays, aps = {}, {}

    def give(name, a):
        arrays[name] = a
        aps[name] = nc.dram_tensor(name, a.shape, mybir.dt.from_np(a.dtype), kind="ExternalInput").ap()

    for name in _INS:
        a = np.ascontiguousarray(inputs[name])
        give(name, a.reshape(DIM, 1) if a.ndim == 1 else a)
    cos_t, sin_t = rope_tables()
    give("cos_table", cos_t)
    give("sin_table", sin_t)
    out = nc.dram_tensor("out", (BATCH, SEQ, DIM), FP32, kind="ExternalOutput").ap()
    a = {n.replace("L0_attn_", "").replace("L0_ffn_", ""): v for n, v in aps.items()}
    build(nc, a["x"], a["cos_table"], a["sin_table"], a["wq"], a["wk"], a["wv"], a["wo"], a["w1"], a["w2"], a["w3"],
          a["ln1_g"], a["ln1_b"], a["ln2_g"], a["ln2_b"], a["theta"], a["phi"], a["theta_noise"], a["phi_noise"], out)
    r = run(nc, [arrays], core_ids=[0])
    return r.results[0]["out"]
```

```python
import math

import concourse.bass as bass
import concourse.mybir as mybir
import numpy as np
from contextlib import ExitStack

FP32 = mybir.dt.float32
BF16 = mybir.dt.bfloat16
ALU = mybir.AluOpType
ACT = mybir.ActivationFunctionType
AX = mybir.AxisListType.X

BATCH, SEQ, DIM = 8, 512, 128
HEADS = 16
HD = DIM // HEADS
HIDDEN = 352
P = 128
TILES = SEQ // P
PAIRS = HEADS // 2
QUADS = HEADS // 4
CHUNKS = [(0, 128), (128, 128), (256, 96)]
EPS = 1e-5
TINY = 1e-19
THETA = 10000.0
SCALE = HD ** -0.5
NEG = -1e30
SLOTS_Q = (0, 0, 0, 1, 1, 2)
SLOTS_K = (0, 1, 2, 0, 1, 0)
SPLIT_ROWS = 16 * len(SLOTS_Q)
SHIFT_ROWS = SPLIT_ROWS + 1
K_DMAS, Q_DMAS = 16 * 3, 16 * 12
A_USES = 7
MAX_AT = ((0, 1), (2,), (3,), (4,), (5, 6), (), (), ())
MAXT_AT = 5
UNITS = 2 * 4 * QUADS


def build(nc, x, cos_t, sin_t, wq, wk, wv, wo, w1, w2, w3, g1, b1, g2, b2,
          theta, phi, theta_n, phi_n, out):
    ctx = ExitStack()
    with ctx:
        def sb(name, shape, dt=FP32):
            return ctx.enter_context(nc.sbuf_tensor(name, shape, dt))

        def sem(name):
            return ctx.enter_context(nc.semaphore(name))

        ident = sb("ident", [P, P])
        ident_b = sb("ident_b", [P, P], BF16)
        band_mask = sb("band_mask", [P, 2, 2 * P], BF16)
        causal_mask = sb("causal_mask", [P, 4, P], BF16)
        cos_sb = sb("cos_sb", [P, SEQ])
        sin_sb = sb("sin_sb", [P, SEQ])
        wqk = sb("wqk", [P, 4, P])
        wv_sb = sb("wv_sb", [P, P])
        wo_sb = sb("wo_sb", [P, P])
        w1_sb = sb("w1_sb", [P, HIDDEN])
        w3_sb = sb("w3_sb", [P, HIDDEN])
        w2_sb = sb("w2_sb", [P, 3, P])
        gb = sb("gb", [P, 4])
        raw = sb("raw", [P, 4, P])
        ang = sb("ang", [P, 2, P])
        turns = sb("turns", [P, 2, P])
        spec_w = sb("spec_w", [P, 2 * P])

        xt = sb("xt", [P, 2, TILES, P])
        f_st = sb("f_st", [P, 2, TILES, 6])
        f_mv = sb("f_mv", [P, 2, TILES, 2])
        f_negm = sb("f_negm", [P, 2, TILES])
        f_ln = sb("f_ln", [P, 3, TILES])
        f_rs = sb("f_rs", [P, 4, TILES])
        f_vyt = sb("f_vyt", [P, 2, TILES])
        eps_ap = sb("eps_ap", [P, 4])
        n0 = sb("n0", [P, TILES, P])
        n0T = sb("n0T", [P, SEQ])
        f_sq = sb("f_sq", [P, TILES, 2 * P])
        f_z = sb("f_z", [P, TILES, P])
        x1 = sb("x1", [P, TILES, P])
        y = sb("y", [P, 2, TILES, P])
        xy = sb("xy", [P, 2, TILES, P])
        yn = sb("yn", [P, TILES, P])
        n1T = sb("n1T", [P, SEQ])
        rot = sb("rot", [P, 2, 2, SEQ])
        roped = sb("roped", [P, 2, SEQ])
        resid = sb("resid", [P, 2, SEQ])
        parts = sb("parts", [P, 2, 3, SEQ], BF16)
        vaug = sb("vaug", [P, 2, TILES, HEADS, 32])
        qz = sb("qz", [P, 2, PAIRS, 2, SEQ], BF16)
        ks = sb("ks", [P, 2, PAIRS, SEQ], BF16)

        mx = sb("mx", [P, 2, 2, 2, TILES])
        mxT = sb("mxT", [16, 2, P], BF16)
        prob = sb("prob", [P, 4, 2, 2, 2 * P])
        o_sb = sb("o_sb", [P, SEQ])
        rden = sb("rden", [P, TILES, 4])
        attn = sb("attn", [P, TILES, P])

        t_st = sb("t_st", [P, 2, TILES, 6])
        t_mv = sb("t_mv", [P, 2, TILES, 2])
        t_negm = sb("t_negm", [P, 2, TILES])
        t_ln = sb("t_ln", [P, 2, TILES])
        t_rs = sb("t_rs", [P, 2, TILES])
        attnT = sb("attnT", [P, SEQ])
        h = sb("h", [P, TILES, P])
        hx1 = sb("hx1", [P, TILES, P])
        n2 = sb("n2", [P, TILES, P])
        n2T = sb("n2T", [P, SEQ])
        up = sb("up", [P, 3, SEQ])
        sg = sb("sg", [P, 5, SEQ])
        act_up = sb("act_up", [P, 3, SEQ])
        gated = sb("gated", [P, 3, SEQ])
        x2 = sb("x2", [P, TILES, P])
        n3 = sb("n3", [P, TILES, P])
        n3T = sb("n3T", [P, SEQ])
        t_sq = sb("t_sq", [P, TILES, 2 * P])
        t_z = sb("t_z", [P, TILES, P])
        x3 = sb("x3", [P, TILES, P])

        s_ps = ctx.enter_context(nc.psum_tensor("s_ps", [P, 3, 512], FP32))
        a_ps = ctx.enter_context(nc.psum_tensor("a_ps", [P, 2, 512], FP32))
        o_ps = ctx.enter_context(nc.psum_tensor("o_ps", [P, 512], FP32))
        f_ps = ctx.enter_context(nc.psum_tensor("f_ps", [P, 512], FP32))
        t_ps = ctx.enter_context(nc.psum_tensor("t_ps", [P, 512], FP32))

        angles_in = sem("angles_in")
        qk_in = sem("qk_in")
        front_in = sem("front_in")
        tail_in = sem("tail_in")
        consts_made = sem("consts_made")
        masks_made = sem("masks_made")
        ones_made = sem("ones_made")
        consts_dve = sem("consts_dve")
        angles = sem("angles")
        angle_step = sem("angle_step")
        spec_ready = sem("spec_ready")
        rot_ready = sem("rot_ready")
        x_in = sem("x_in")
        x_stats = sem("x_stats")
        x_mv = sem("x_mv")
        x_negm = sem("x_negm")
        x_lnvar = sem("x_lnvar")
        x_rstd = sem("x_rstd")
        n0_ready = sem("n0_ready")
        early_mm = sem("early_mm")
        early_act = sem("early_act")
        front_mm = sem("front_mm")
        front_read = sem("front_read")
        z1_ready = sem("z1_ready")
        lnz1 = sem("lnz1")
        mag1 = sem("mag1")
        x1_ready = sem("x1_ready")
        x1_stats = sem("x1_stats")
        x1_mv = sem("x1_mv")
        x1_negm = sem("x1_negm")
        x1_lnvar = sem("x1_lnvar")
        x1_rstd = sem("x1_rstd")
        vy_part = sem("vy_part")
        vy_ready = sem("vy_ready")
        vy_ln = sem("vy_ln")
        vy_rstd = sem("vy_rstd")
        rs2_ready = sem("rs2_ready")
        y_ready = sem("y_ready")
        xy_ready = sem("xy_ready")
        yn_ready = sem("yn_ready")
        roped_ready = sem("roped_ready")
        high_ready = sem("high_ready")
        resid_q = sem("resid_q")
        resid_k = sem("resid_k")
        mid_ready = sem("mid_ready")
        low_q = sem("low_q")
        low_k = sem("low_k")
        q_spilled = sem("q_spilled")
        k_spilled = sem("k_spilled")
        k_stacked = sem("k_stacked")
        q_stacked = sem("q_stacked")
        max_scores = sem("max_scores")
        max_done = sem("max_done")
        maxT_mm = sem("maxT_mm")
        maxT_out = sem("maxT_out")
        shift_in = sem("shift_in")
        scores = sem("scores")
        exp_done = sem("exp_done")
        masked = sem("masked")
        pv_done = sem("pv_done")
        o_out = sem("o_out")
        oT_mm = sem("oT_mm")
        den_done = sem("den_done")
        attn_done = sem("attn_done")
        tail_mm = sem("tail_mm")
        tail_read = sem("tail_read")
        late_mm = sem("late_mm")
        late_act = sem("late_act")
        h_stats = sem("h_stats")
        h_mv = sem("h_mv")
        h_negm = sem("h_negm")
        h_lnvar = sem("h_lnvar")
        h_rstd = sem("h_rstd")
        n2_ready = sem("n2_ready")
        silu_e = sem("silu_e")
        silu_l = sem("silu_l")
        silu_s = sem("silu_s")
        silu_u = sem("silu_u")
        x2_stats = sem("x2_stats")
        x2_mv = sem("x2_mv")
        x2_negm = sem("x2_negm")
        x2_lnvar = sem("x2_lnvar")
        x2_rstd = sem("x2_rstd")
        n3_ready = sem("n3_ready")
        z2_ready = sem("z2_ready")
        lnz2 = sem("lnz2")
        mag2 = sem("mag2")
        x3_ready = sem("x3_ready")
        stored = sem("stored")
        waits_passed = sem("waits_passed")

        q_dram = nc.dram_tensor("q_dram", (3, P, SEQ), BF16).ap()
        k_dram = nc.dram_tensor("k_dram", (PAIRS, 3, 16, SEQ), BF16).ap()

        SPEC_BANKS = (a_ps[:, 0, :], a_ps[:, 1, :])
        FIRST_BANKS = (f_ps[:, :], s_ps[:, 0, :], s_ps[:, 1, :], s_ps[:, 2, :])
        LAST_BANKS = (s_ps[:, 0, :], s_ps[:, 1, :], s_ps[:, 2, :], a_ps[:, 0, :], a_ps[:, 1, :], f_ps[:, :])

        block = ctx.enter_context(nc.Block())
        last = BATCH - 1

        def wait_alone(eng, s, n):
            eng.wait_ge(s, n)
            eng.sem_inc(waits_passed, 1)

        def batches(eng, first, body, tail):
            def peeled(b):
                body(b, b % 2, b + 2 <= last, b + 1 <= last, b >= 1, b >= 2)

            first()
            peeled(0)
            peeled(1)
            with eng.Fori(1, BATCH // 2 - 1) as pair:
                body(2 * pair, 0, True, True, True, True)
                body(2 * pair + 1, 1, True, True, True, True)
            peeled(last - 1)
            peeled(last)
            tail()

        @block.sync
        def _(sp):
            loads = (
                (angles_in, raw[:, 0, :], theta), (angles_in, raw[:, 1, :], theta_n),
                (angles_in, raw[:, 2, :], phi), (angles_in, raw[:, 3, :], phi_n),
                (qk_in, wqk[:, 0, :], wq), (qk_in, wqk[:, 2, :], wk),
                (front_in, gb[:, 0:1], g1), (front_in, gb[:, 1:2], b1),
                (front_in, gb[:, 2:3], g2), (front_in, gb[:, 3:4], b2),
                (front_in, cos_sb[:, :], cos_t), (front_in, sin_sb[:, :], sin_t), (front_in, wv_sb[:, :], wv),
                (tail_in, wo_sb[:, :], wo), (tail_in, w1_sb[:, :], w1), (tail_in, w3_sb[:, :], w3),
                (tail_in, w2_sb[:, 0:2, :], w2[0:256, :].rearrange("(c p) d -> p c d", p=P)),
                (tail_in, w2_sb[0:96, 2, :], w2[256:352, :]),
            )

            sp.sem_inc(stored, 16)

            def load_x(f, p):
                if not (isinstance(f, int) and f < 2):
                    wait_alone(sp, x1_ready, f - 1)
                if not (isinstance(f, int) and f < 1):
                    wait_alone(sp, x_in, 16 * f)
                sp.dma_start(xt[:, p, :, :], x[f].rearrange("(t p) d -> p t d", p=P)).then_inc(x_in, 16)

            def stack(f, p):
                if not (isinstance(f, int) and f < 1):
                    wait_alone(sp, q_stacked, Q_DMAS * f)
                    wait_alone(sp, k_stacked, K_DMAS * f)
                def spill_q(part, s, n):
                    sp.wait_ge(s, n)
                    sp.dma_start(q_dram[part], parts[:, 0, part, :]).then_inc(q_spilled, 16)

                def spill_k(part, s, n):
                    sp.wait_ge(s, n)
                    sp.dma_start(k_dram[:, part], parts[:, 1, part, :]).then_inc(k_spilled, 16)

                def stack_q(part):
                    wait_alone(sp, q_spilled, 48 * f + 16 * (part + 1))
                    if part == 0 and not (isinstance(f, int) and f < 2):
                        sp.wait_ge(pv_done, 16 * (f - 1))
                    src = q_dram[part].rearrange("(s g d) n -> g d s n", g=2, d=HD)
                    for j in range(len(SLOTS_Q)):
                        for g in range(2) if SLOTS_Q[j] == part else ():
                            sp.dma_start(qz[16 * j + 8 * g:16 * j + 8 * g + 8, p, :, g, :], src[g]).then_inc(q_stacked, 16)

                spill_q(0, high_ready, 2 * f + 1)
                stack_q(0)
                spill_q(1, mid_ready, 2 * f + 1)
                spill_k(0, high_ready, 2 * f + 2)
                stack_q(1)
                spill_q(2, low_q, f + 1)
                spill_k(1, mid_ready, 2 * f + 2)
                spill_k(2, low_k, f + 1)
                stack_q(2)
                sp.wait_ge(k_spilled, 48 * (f + 1))
                for row, n in ((0, 3), (48, 2), (80, 1)):
                    sp.dma_start(ks[row:row + 16 * n, p, :, :],
                                 k_dram[:, 0:n].rearrange("s a r n -> (a r) s n")).then_inc(k_stacked, 16)

            def store(w):
                wait_alone(sp, x3_ready, w + 1)
                sp.dma_start(out[w].rearrange("(t p) d -> p t d", p=P), x3[:, :, :]).then_inc(stored, 16)

            def step(f, p):
                if not (isinstance(f, int) and f == last):
                    load_x(f + 1, 1 - p)
                stack(f, p)
                if not (isinstance(f, int) and f < 3):
                    store(f - 3)

            load_x(0, 0)
            for done, dst, src in loads:
                sp.dma_start(dst, src).then_inc(done, 16)
            wait_alone(sp, consts_dve, 5)
            wait_alone(sp, ones_made, 2)
            for f in range(3):
                step(f, f % 2)
            with sp.Fori(1, BATCH // 2 - 1) as pair:
                step(2 * pair + 1, 1)
                step(2 * pair + 2, 0)
            step(last, 1)
            for w in range(BATCH - 3, BATCH):
                store(w)
            sp.wait_ge(stored, 16 * BATCH + 16)

        @block.gpsimd
        def _(pool):
            for n, (t, v) in enumerate(((ident, 0.0), (ident_b, 0.0), (band_mask, 0.0), (causal_mask, 0.0))):
                nc.gpsimd.memset(t[:], v).then_inc(consts_made, 1)
            pool.wait_ge(consts_made, 4)
            for t in (ident, ident_b):
                nc.gpsimd.affine_select(out=t[:, :], in_=t[:, :], compare_op=ALU.not_equal, fill=1.0, base=0,
                                        pattern=[[-1, P]], channel_multiplier=1).then_inc(masks_made, 1)
            nc.gpsimd.affine_select(out=causal_mask[:], in_=causal_mask[:], compare_op=ALU.is_ge, fill=NEG, base=0,
                                    pattern=[[0, 4], [-1, P]], channel_multiplier=1).then_inc(masks_made, 1)
            nc.gpsimd.affine_select(out=band_mask[:], in_=band_mask[:], compare_op=ALU.is_ge, fill=NEG, base=0,
                                    pattern=[[0, 2], [1, 2 * P]], channel_multiplier=-1).then_inc(consts_made, 1)
            pool.wait_ge(consts_made, 5)
            nc.gpsimd.affine_select(out=band_mask[:], in_=band_mask[:], compare_op=ALU.is_ge, fill=NEG, base=P,
                                    pattern=[[0, 2], [-1, 2 * P]], channel_multiplier=1).then_inc(masks_made, 1)

            def ones():
                nc.gpsimd.memset(ks[:], 1.0).then_inc(ones_made, 1)
                nc.gpsimd.memset(vaug[:], 1.0).then_inc(ones_made, 1)

            def norm(dst, src, negm, rs, done):
                for t in range(TILES):
                    ins = nc.gpsimd.tensor_scalar(dst[:, t, :], src[:, t, :], negm[:, t:t + 1], rs[:, t:t + 1],
                                                  ALU.add, ALU.mult)
                ins.then_inc(done, 1)

            def f_n0(f, p):
                pool.wait_ge(x_rstd, f + 1)
                wait_alone(pool, x_negm, f + 1)
                norm(n0, xt[:, p], f_negm[:, 0], f_rs[:, 0], n0_ready)

            def f_yn(f):
                pool.wait_ge(rs2_ready, f + 1)
                wait_alone(pool, x1_negm, f + 1)
                norm(yn, x1, f_negm[:, 1], f_rs[:, 3], yn_ready)

            def f_y(f, p):
                norm(y[:, p], x1, f_negm[:, 1], f_rs[:, 1], y_ready)

            def f_xy(f, p):
                pool.wait_ge(y_ready, f + 1)
                nc.gpsimd.tensor_tensor(xy[:, p, :, :], x1[:, :, :], y[:, p, :, :], ALU.add).then_inc(xy_ready, 1)

            def f_rope(f, i):
                pool.wait_ge(front_read, 6 * f + 3 + 2 * i)
                nc.gpsimd.tensor_tensor(roped[:, i, :], rot[:, i, 0, :], rot[:, i, 1, :], ALU.add).then_inc(roped_ready, 1)

            def f_resid_q(f):
                pool.wait_ge(high_ready, 2 * f + 1)
                nc.gpsimd.tensor_tensor(resid[:, 0, :], roped[:, 0, :], parts[:, 0, 0, :], ALU.subtract).then_inc(resid_q, 1)

            def f_low_q(f):
                pool.wait_ge(mid_ready, 2 * f + 1)
                pool.wait_ge(resid_q, f + 1)
                nc.gpsimd.tensor_tensor(parts[:, 0, 2, :], resid[:, 0, :], parts[:, 0, 1, :], ALU.subtract).then_inc(low_q, 1)

            def mask(b, s):
                kt = s % 4
                wait_alone(pool, exp_done, 32 * b + 2 * s + 2)
                own = prob[:, s % 4, :, :, 0:P].rearrange("p a g n -> p (a g) n")
                ins = nc.gpsimd.affine_select(out=own, in_=own, compare_op=ALU.is_ge, fill=0.0, base=0,
                                              pattern=[[0, 4], [1, P]], channel_multiplier=-1)
                if kt < 3:
                    nxt = prob[:, s % 4, :, :, P:2 * P].rearrange("p a g n -> p (a g) n")
                    ins = nc.gpsimd.affine_select(out=nxt, in_=nxt, compare_op=ALU.is_ge, fill=0.0, base=0,
                                                  pattern=[[0, 4], [-1, P]], channel_multiplier=1)
                ins.then_inc(masked, 1)

            def t_n2(w):
                pool.wait_ge(h_rstd, w + 1)
                wait_alone(pool, h_negm, w + 1)
                norm(n2, h, t_negm[:, 0], t_rs[:, 0], n2_ready)

            def t_u(w, c):
                pool.wait_ge(silu_s, 3 * w + c + 1)
                r = CHUNKS[c][1]
                nc.gpsimd.tensor_tensor(act_up[0:r, c, :], up[0:r, c, :], sg[0:r, 2 + c, :], ALU.mult).then_inc(silu_u, 1)

            def t_n3(w):
                pool.wait_ge(x2_rstd, w + 1)
                wait_alone(pool, x2_negm, w + 1)
                norm(n3, x2, t_negm[:, 1], t_rs[:, 1], n3_ready)

            def first():
                ones()
                f_rope(0, 0)
                f_resid_q(0)
                f_rope(0, 1)
                f_low_q(0)
                wait_alone(pool, x1_negm, 1)
                f_y(0, 0)
                f_xy(0, 0)
                f_n0(1, 1)

            def body(b, p, has_early, has_front, has_tail, has_late):
                f, w = b + 1, b - 1
                for h in range(UNITS):
                    if h % 2 == 1:
                        mask(b, h // 2)
                    if has_tail:
                        if h == 8:
                            t_n2(w)
                        if h in (13, 15, 17):
                            t_u(w, (h - 13) // 2)
                    if has_early:
                        if h == 16:
                            f_n0(b + 2, p)
                    if has_late:
                        if h == 4:
                            t_n3(b - 2)
                    if has_front:
                        if h == 0:
                            f_yn(f)
                        if h == 9:
                            f_rope(f, 0)
                        if h == 11:
                            f_resid_q(f)
                            f_rope(f, 1)
                        if h == 13:
                            f_low_q(f)
                        if h == 22:
                            f_y(f, 1 - p)
                        if h == 24:
                            f_xy(f, 1 - p)

            def tail():
                t_n3(last - 1)
                for c in range(3):
                    t_u(last, c)

            batches(pool, first, body, tail)

        @block.scalar
        def _(act):
            def spectral_weights():
                act.wait_ge(angles, 6)
                nc.scalar.activation(spec_w[:, 0:P], ang[:, 0, :], ACT.Sin).then_inc(spec_ready, 1)
                nc.scalar.activation(spec_w[:, P:2 * P], ang[:, 1, :], ACT.Sin).then_inc(spec_ready, 1)

            def rsqrt(dst, tmp, var, lnsem, done, n):
                nc.scalar.activation(tmp, var, ACT.Ln, bias=eps_ap[:, 0:1]).then_inc(lnsem, 1)
                act.wait_ge(lnsem, n)
                nc.scalar.activation(dst, tmp, ACT.Exp, scale=-0.5).then_inc(done, 1)

            def magnitude(dst, tmp, z, lnsem, done, n):
                nc.scalar.activation(tmp, z, ACT.Ln, bias=eps_ap[:, 1:2]).then_inc(lnsem, 1)
                act.wait_ge(lnsem, n)
                nc.scalar.activation(dst, tmp, ACT.Exp, scale=0.5, bias=eps_ap[:, 2:3]).then_inc(done, 1)

            def f_rs0(f):
                act.wait_ge(x_mv, f + 1)
                rsqrt(f_rs[:, 0, :], f_ln[:, 0, :], f_mv[:, 0, :, 1], x_lnvar, x_rstd, f + 1)

            def f_n0T(f):
                act.wait_ge(early_mm, 3 * f + 1)
                nc.scalar.activation(n0T[:, :], f_ps[:, :], ACT.Copy).then_inc(early_act, 1)

            def f_square(f, half, bank=None):
                act.wait_ge(early_mm, 3 * f + 2 + half)
                nc.scalar.activation(f_sq[:, 2 * half:2 * half + 2, :].rearrange("p t n -> p (t n)"),
                                     f_ps[:, :] if bank is None else bank, ACT.Square).then_inc(early_act, 1)

            def f_mag1(f):
                act.wait_ge(z1_ready, f + 1)
                magnitude(f_z[:, :, :], f_z[:, :, :], f_z[:, :, :], lnz1, mag1, f + 1)

            def f_rs1(f):
                act.wait_ge(x1_mv, f + 1)
                rsqrt(f_rs[:, 1, :], f_ln[:, 1, :], f_mv[:, 1, :, 1], x1_lnvar, x1_rstd, f + 1)

            def f_rs2(f):
                act.wait_ge(vy_ready, f + 1)
                rsqrt(f_rs[:, 2, :], f_ln[:, 2, :], f_vyt[:, 1, :], vy_ln, vy_rstd, f + 1)

            def f_n1T(f):
                act.wait_ge(front_mm, 6 * f + 1)
                nc.scalar.activation(n1T[:, :], f_ps[:, :], ACT.Identity, scale=gb[:, 0:1],
                                     bias=gb[:, 1:2]).then_inc(front_read, 1)

            def f_v(f, p):
                act.wait_ge(front_mm, 6 * f + 6)
                if not (isinstance(f, int) and f < 2):
                    act.wait_ge(pv_done, 16 * (f - 1))
                nc.scalar.activation(vaug[:, p, :, :, 0:HD].rearrange("p t h d -> p (t h) d"),
                                     f_ps[:, :].rearrange("p (a d) -> p a d", d=HD), ACT.Copy).then_inc(front_read, 1)

            def f_high(f, i):
                act.wait_ge(roped_ready, 2 * f + i + 1)
                if not (isinstance(f, int) and f < 1):
                    act.wait_ge(k_spilled if i else q_spilled, 48 * f)
                nc.scalar.activation(parts[:, i, 0, :], roped[:, i, :], ACT.Copy).then_inc(high_ready, 1)

            def f_mid(f, i):
                act.wait_ge(resid_k if i else resid_q, f + 1)
                nc.scalar.activation(parts[:, i, 1, :], resid[:, i, :], ACT.Copy).then_inc(mid_ready, 1)

            def maxT(a, c):
                act.wait_ge(maxT_mm, 4 * a + c + 1)
                if not (isinstance(a, int) and 4 * a + c < 2):
                    act.wait_ge(shift_in, 16 * (4 * a + c - 1))
                nc.scalar.activation(mxT[:, c % 2, :], a_ps[0:16, 1, 0:P], ACT.Copy, scale=-1.0).then_inc(maxT_out, 1)

            def shift(a, p, c):
                act.wait_ge(maxT_out, 4 * a + c + 1)
                dst = qz[SPLIT_ROWS:SHIFT_ROWS, p, 2 * c:2 * c + 2, :, :].rearrange("o s g n -> o (s g n)")
                act.dma_start(dst, mxT[:, c % 2, :]).then_inc(shift_in, 16)

            def exp(b, v):
                kt = (v % 8) // 2
                act.wait_ge(scores, 32 * b + v + 1)
                if not (isinstance(b, int) and 16 * b + v // 2 < 4):
                    act.wait_ge(pv_done, 16 * b + v // 2 - 3)
                n = 2 * P if kt < 3 else P
                bank = s_ps[:, v % 3, 0:2 * n].rearrange("p (g n) -> p g n", g=2)
                nc.scalar.activation(prob[:, (v // 2) % 4, v % 2, :, 0:n], bank, ACT.Exp, scale=SCALE).then_inc(exp_done, 1)

            def o_copy(b, c):
                act.wait_ge(pv_done, 16 * b + 4 * c + 4)
                nc.scalar.activation(o_sb[:, :], o_ps[:, :], ACT.Copy).then_inc(o_out, 1)

            def t_attnT(w):
                act.wait_ge(tail_mm, 10 * w + 1)
                nc.scalar.activation(attnT[:, :], t_ps[:, :], ACT.Copy).then_inc(tail_read, 1)

            def t_rs0(w):
                act.wait_ge(h_mv, w + 1)
                rsqrt(t_rs[:, 0, :], t_ln[:, 0, :], t_mv[:, 0, :, 1], h_lnvar, h_rstd, w + 1)

            def t_sig(w, c):
                r = CHUNKS[c][1]
                act.wait_ge(tail_read, 10 * w + 4 + c)
                nc.scalar.activation(sg[0:r, 0, :], up[0:r, c, :], ACT.Exp, scale=-1.0).then_inc(silu_e, 1)
                act.wait_ge(silu_e, 3 * w + c + 1)
                nc.scalar.activation(sg[0:r, 1, :], sg[0:r, 0, :], ACT.Ln, bias=eps_ap[0:r, 3:4]).then_inc(silu_l, 1)
                act.wait_ge(silu_l, 3 * w + c + 1)
                nc.scalar.activation(sg[0:r, 2 + c, :], sg[0:r, 1, :], ACT.Exp, scale=-1.0).then_inc(silu_s, 1)

            def t_rs1(w):
                act.wait_ge(x2_mv, w + 1)
                rsqrt(t_rs[:, 1, :], t_ln[:, 1, :], t_mv[:, 1, :, 1], x2_lnvar, x2_rstd, w + 1)

            def t_n3T(w):
                act.wait_ge(late_mm, 3 * w + 1)
                nc.scalar.activation(n3T[:, :], t_ps[:, :], ACT.Copy).then_inc(late_act, 1)

            def t_square(w, half, bank=None):
                act.wait_ge(late_mm, 3 * w + 2 + half)
                nc.scalar.activation(t_sq[:, 2 * half:2 * half + 2, :].rearrange("p t n -> p (t n)"),
                                     t_ps[:, :] if bank is None else bank, ACT.Square).then_inc(late_act, 1)

            def t_mag2(w):
                act.wait_ge(z2_ready, w + 1)
                magnitude(t_z[:, :, :], t_z[:, :, :], t_z[:, :, :], lnz2, mag2, w + 1)

            def first():
                for f in range(2):
                    if f == 0:
                        act.preload_act_table_set("natural_log_exp_and_others")
                    f_rs0(f)
                    if f == 0:
                        spectral_weights()
                        act.preload_act_table_set("natural_log_exp_and_others")
                    f_n0T(f)
                    f_square(f, 0, SPEC_BANKS[0])
                    f_square(f, 1, SPEC_BANKS[1])
                    f_mag1(f)
                    if f == 0:
                        f_rs1(0)
                        f_rs2(0)
                        act.wait_ge(front_in, 16 * 7)
                        f_n1T(0)
                        f_high(0, 0)
                        f_mid(0, 0)
                        f_high(0, 1)
                        act.wait_ge(ones_made, 2)
                        f_v(0, 0)
                        f_mid(0, 1)
                maxT(0, 0)
                shift(0, 0, 0)
                f_rs1(1)
                f_rs2(1)

            def body(b, p, has_early, has_front, has_tail, has_late):
                f, w = b + 1, b - 1
                for h in range(UNITS):
                    exp(b, h)
                    if h == 2 and has_tail:
                        o_copy(w, 3)
                    if h in (10, 18, 26):
                        o_copy(b, h // 8 - 1)
                    if h < 24 and h % 8 == MAXT_AT:
                        maxT(b, h // 8 + 1)
                        shift(b, p, h // 8 + 1)
                    if h == 24 + MAXT_AT and has_front:
                        maxT(f, 0)
                        shift(f, 1 - p, 0)
                    if has_tail:
                        if h == 4:
                            t_attnT(w)
                        if h == 7:
                            t_rs0(w)
                    if has_late:
                        if h == 7:
                            t_n3T(b - 2)
                        if h in (8, 9):
                            t_square(b - 2, h - 8)
                        if h == 19:
                            t_mag2(b - 2)
                    if has_front:
                        if h == 3:
                            f_n1T(f)
                        if h == 11:
                            f_v(f, 1 - p)
                        if h == 10:
                            f_high(f, 0)
                        if h == 12:
                            f_mid(f, 0)
                        if h == 13:
                            f_high(f, 1)
                        if h == 15:
                            f_mid(f, 1)
                    if has_tail:
                        if h in (12, 14, 16):
                            t_sig(w, (h - 12) // 2)
                        if h == 24:
                            t_rs1(w)
                    if has_early:
                        if h == 14:
                            f_rs0(b + 2)
                        if h == 18:
                            f_n0T(b + 2)
                        if h in (19, 20):
                            f_square(b + 2, h - 19)
                        if h == 22:
                            f_mag1(b + 2)
                        if h == 30:
                            f_rs1(b + 2)
                        if h == 31:
                            f_rs2(b + 2)

            def tail():
                o_copy(last, 3)
                t_attnT(last)
                t_n3T(last - 1)
                t_rs0(last)
                t_square(last - 1, 0, SPEC_BANKS[0])
                t_square(last - 1, 1, SPEC_BANKS[1])
                for c in range(3):
                    t_sig(last, c)
                t_mag2(last - 1)
                t_rs1(last)
                t_n3T(last)
                t_square(last, 0, SPEC_BANKS[0])
                t_square(last, 1, SPEC_BANKS[1])
                t_mag2(last)

            batches(act, first, body, tail)

        @block.vector
        def _(dve):
            for i, v in enumerate((EPS, TINY, math.log(0.5), 1.0)):
                nc.vector.memset(eps_ap[:, i:i + 1], v).then_inc(consts_dve, 1)

            def angles_and_rotations():
                dve.wait_ge(angles_in, 16 * 4)
                nc.vector.tensor_tensor(ang[:, 0, :], raw[:, 0, :], raw[:, 1, :], ALU.add).then_inc(angles, 1)
                nc.vector.tensor_tensor(ang[:, 1, :], raw[:, 2, :], raw[:, 3, :], ALU.add).then_inc(angles, 1)
                dve.wait_ge(angles, 2)
                nc.vector.tensor_scalar(ang[:, 0, :], ang[:, 0, :], math.pi / 2, None, ALU.add).then_inc(angle_step, 1)
                dve.wait_ge(angle_step, 1)
                big = 1.5 * 2 ** 23
                nc.vector.tensor_scalar(turns[:], ang[:], 1 / (2 * math.pi), big, ALU.mult, ALU.add).then_inc(angle_step, 1)
                dve.wait_ge(angle_step, 2)
                nc.vector.tensor_scalar(turns[:], turns[:], big, None, ALU.subtract).then_inc(angle_step, 1)
                dve.wait_ge(angle_step, 3)
                nc.vector.scalar_tensor_tensor(out=ang[:], in0=turns[:], scalar=-6.28125, in1=ang[:],
                                               op0=ALU.mult, op1=ALU.add).then_inc(angle_step, 1)
                dve.wait_ge(angle_step, 4)
                nc.vector.scalar_tensor_tensor(out=ang[:], in0=turns[:], scalar=-(2 * math.pi - 6.28125), in1=ang[:],
                                               op0=ALU.mult, op1=ALU.add).then_inc(angle_step, 1)
                dve.wait_ge(angle_step, 5)
                nc.vector.tensor_scalar(ang[:], ang[:], float(np.float32(3.1415925)), -float(np.float32(3.1415925)),
                                        ALU.min, ALU.max).then_inc(angles, 4)
                dve.wait_ge(qk_in, 16 * 2)
                for i in (0, 2):
                    src = wqk[:, i, :].rearrange("p (j e) -> p j e", e=2)
                    dst = wqk[:, i + 1, :].rearrange("p (j e) -> p j e", e=2)
                    nc.vector.tensor_scalar(dst[:, :, 0], src[:, :, 1], -1.0, None, ALU.mult).then_inc(rot_ready, 1)
                    nc.vector.tensor_copy(dst[:, :, 1], src[:, :, 0]).then_inc(rot_ready, 1)

            def stats(src, st, mv, negm, s_st, s_mv, s_neg, n):
                for t in range(TILES):
                    ins = nc.vector.bn_stats(st[:, t, :], src[:, t, :])
                ins.then_inc(s_st, 1)
                wait_alone(dve, s_st, n)
                for t in range(TILES):
                    ins = nc.vector.bn_aggr(mv[:, t, :], st[:, t, :])
                ins.then_inc(s_mv, 1)
                dve.wait_ge(s_mv, n)
                nc.vector.tensor_scalar(negm, mv[:, :, 0], -1.0, None, ALU.mult).then_inc(s_neg, 1)

            def norm(dst, src, negm, rs, negm_sem, rs_sem, done, n):
                dve.wait_ge(rs_sem, n)
                wait_alone(dve, negm_sem, n)
                for t in range(TILES):
                    ins = nc.vector.tensor_scalar(dst[:, t, :], src[:, t, :], negm[:, t:t + 1], rs[:, t:t + 1],
                                                  ALU.add, ALU.mult)
                ins.then_inc(done, 1)

            def f_stats0(f, p):
                dve.wait_ge(x_in, 16 * (f + 1))
                stats(xt[:, p], f_st[:, 0], f_mv[:, 0], f_negm[:, 0, :], x_stats, x_mv, x_negm, f + 1)

            def f_z1(f):
                dve.wait_ge(early_act, 3 * f + 3)
                nc.vector.tensor_tensor(f_z[:, :, :], f_sq[:, :, 0:P], f_sq[:, :, P:2 * P], ALU.add).then_inc(z1_ready, 1)

            def f_x1(f, p):
                dve.wait_ge(mag1, f + 1)
                if not (isinstance(f, int) and f < 1):
                    wait_alone(dve, xy_ready, f)
                nc.vector.tensor_tensor(x1[:, :, :], xt[:, p, :, :], f_z[:, :, :], ALU.add).then_inc(x1_ready, 1)
                dve.wait_ge(x1_ready, f + 1)
                stats(x1, f_st[:, 1], f_mv[:, 1], f_negm[:, 1, :], x1_stats, x1_mv, x1_negm, f + 1)

            def f_vy(f):
                dve.wait_ge(x1_rstd, f + 1)
                nc.vector.tensor_tensor(f_vyt[:, 0, :], f_mv[:, 1, :, 1], f_rs[:, 1, :], ALU.mult).then_inc(vy_part, 1)
                dve.wait_ge(vy_part, f + 1)
                nc.vector.tensor_tensor(f_vyt[:, 1, :], f_vyt[:, 0, :], f_rs[:, 1, :], ALU.mult).then_inc(vy_ready, 1)

            def f_rs2(f):
                dve.wait_ge(vy_rstd, f + 1)
                nc.vector.tensor_tensor(f_rs[:, 3, :], f_rs[:, 1, :], f_rs[:, 2, :], ALU.mult).then_inc(rs2_ready, 1)

            def f_rot(f, i, j, bank=None):
                dve.wait_ge(front_mm, 6 * f + 2 + 2 * i + j)
                nc.vector.tensor_tensor(rot[:, i, j, :], f_ps[:, :] if bank is None else bank, (sin_sb if j else cos_sb)[:, :], ALU.mult).then_inc(front_read, 1)

            def f_resid_k(f):
                dve.wait_ge(high_ready, 2 * f + 2)
                nc.vector.tensor_tensor(resid[:, 1, :], roped[:, 1, :], parts[:, 1, 0, :], ALU.subtract).then_inc(resid_k, 1)

            def f_low_k(f):
                dve.wait_ge(mid_ready, 2 * f + 2)
                nc.vector.tensor_tensor(parts[:, 1, 2, :], resid[:, 1, :], parts[:, 1, 1, :], ALU.subtract).then_inc(low_k, 1)

            def amax(a, c, j):
                dve.wait_ge(max_scores, A_USES * (4 * a + c) + j + 1)
                bank = a_ps[:, j % 2, :]
                if j == 0:
                    dst = mx[:, c % 2, :, :, 0]
                    src = bank.rearrange("p (s g n) -> p s g n", s=2, g=2)
                else:
                    t, pr = (j + 1) // 2, (j + 1) % 2
                    dst, src = mx[:, c % 2, pr, :, t], bank.rearrange("p (g n) -> p g n", g=2)
                nc.vector.tensor_reduce(dst, src, AX, ALU.max).then_inc(max_done, 1)

            def o_norm(b, c):
                dve.wait_ge(oT_mm, 4 * b + c + 1)
                oT = o_ps[:, :].rearrange("p (t h n) -> p t h n", t=TILES, h=4)
                nc.vector.reciprocal(rden[:, :, :], oT[:, :, :, HD]).then_inc(den_done, 1)
                dve.wait_ge(den_done, 4 * b + c + 1)
                if c == 0 and not (isinstance(b, int) and b < 1):
                    dve.wait_ge(tail_mm, 10 * (b - 1) + 1)
                for t in range(TILES):
                    dst = attn[:, t, 32 * c:32 * c + 32].rearrange("p (h d) -> p h d", h=4)
                    ins = nc.vector.tensor_tensor(dst, oT[:, t, :, 0:HD],
                                                  rden[:, t, :].unsqueeze(2).to_broadcast([P, 4, HD]), ALU.mult)
                ins.then_inc(attn_done, 1)

            def t_h(w, p):
                wait_alone(dve, xy_ready, w + 1)
                dve.wait_ge(tail_mm, 10 * w + 2)
                nc.vector.tensor_tensor(h[:, :, :], t_ps[:, :].rearrange("p (t n) -> p t n", t=TILES),
                                        y[:, p, :, :], ALU.add)
                nc.vector.tensor_tensor(hx1[:, :, :], t_ps[:, :].rearrange("p (t n) -> p t n", t=TILES),
                                        xy[:, p, :, :], ALU.add).then_inc(tail_read, 1)
                dve.wait_ge(tail_read, 10 * w + 2)
                stats(h, t_st[:, 0], t_mv[:, 0], t_negm[:, 0, :], h_stats, h_mv, h_negm, w + 1)

            def t_n2T(w):
                dve.wait_ge(tail_mm, 10 * w + 3)
                nc.vector.tensor_scalar(n2T[:, :], t_ps[:, :], gb[:, 2:3], gb[:, 3:4], ALU.mult, ALU.add).then_inc(tail_read, 1)

            def t_up(w, c, bank=None):
                r = CHUNKS[c][1]
                dve.wait_ge(tail_mm, 10 * w + 4 + c)
                nc.vector.tensor_scalar(up[0:r, c, :], (t_ps if bank is None else bank)[0:r, :], -43.0, None, ALU.max).then_inc(tail_read, 1)

            def t_gate(w, c, bank=None):
                r = CHUNKS[c][1]
                dve.wait_ge(tail_mm, 10 * w + 7 + c)
                dve.wait_ge(silu_u, 3 * w + c + 1)
                nc.vector.tensor_tensor(gated[0:r, c, :], (t_ps if bank is None else bank)[0:r, :], act_up[0:r, c, :], ALU.mult).then_inc(tail_read, 1)

            def t_x2(w):
                dve.wait_ge(tail_mm, 10 * w + 10)
                if not (isinstance(w, int) and w < 1):
                    dve.wait_ge(x3_ready, w)
                nc.vector.tensor_tensor(x2[:, :, :], t_ps[:, :].rearrange("p (t n) -> p t n", t=TILES),
                                        hx1[:, :, :], ALU.add).then_inc(tail_read, 1)
                dve.wait_ge(tail_read, 10 * w + 10)
                stats(x2, t_st[:, 1], t_mv[:, 1], t_negm[:, 1, :], x2_stats, x2_mv, x2_negm, w + 1)

            def t_z2(w):
                dve.wait_ge(late_act, 3 * w + 3)
                nc.vector.tensor_tensor(t_z[:, :, :], t_sq[:, :, 0:P], t_sq[:, :, P:2 * P], ALU.add).then_inc(z2_ready, 1)

            def t_x3(w):
                dve.wait_ge(mag2, w + 1)
                dve.wait_ge(stored, 16 * w + 16)
                nc.vector.tensor_tensor(x3[:, :, :], x2[:, :, :], t_z[:, :, :], ALU.add).then_inc(x3_ready, 1)

            def first():
                f_stats0(0, 0)
                angles_and_rotations()
                norm(n0, xt[:, 0], f_negm[:, 0], f_rs[:, 0], x_negm, x_rstd, n0_ready, 1)
                nc.vector.memset(qz[:], 0.0).then_inc(consts_dve, 1)
                f_z1(0)
                f_x1(0, 0)
                f_vy(0)
                f_rs2(0)
                norm(yn, x1, f_negm[:, 1], f_rs[:, 3], x1_negm, rs2_ready, yn_ready, 1)
                dve.wait_ge(front_in, 16 * 7)
                for i in range(4):
                    f_rot(0, i // 2, i % 2, FIRST_BANKS[i])
                f_resid_k(0)
                f_low_k(0)
                f_stats0(1, 1)
                f_z1(1)
                for j in range(A_USES):
                    amax(0, 0, j)
                f_x1(1, 1)
                f_vy(1)
                f_rs2(1)

            def body(b, p, has_early, has_front, has_tail, has_late):
                f, w = b + 1, b - 1
                for h in range(UNITS):
                    c, k = divmod(h, 8)
                    uses = MAX_AT[k] if c < 3 or has_front else ()
                    a = (b, c + 1) if c < 3 else (f, 0)
                    for j in uses[0:1]:
                        amax(*a, j)
                    if h == 3 and has_tail:
                        o_norm(w, 3)
                    if h in (11, 19, 27):
                        o_norm(b, h // 8 - 1)
                    if has_late:
                        if h == 15:
                            t_z2(b - 2)
                        if h == 21:
                            t_x3(b - 2)
                    if has_tail:
                        if h == 5:
                            t_h(w, 1 - p)
                        if h == 10:
                            t_n2T(w)
                        if h in (11, 12, 13):
                            t_up(w, h - 11)
                        if h in (15, 17, 19):
                            t_gate(w, (h - 15) // 2)
                        if h == 22:
                            t_x2(w)
                    for j in uses[1:]:
                        amax(*a, j)
                    if has_front:
                        if h in (7, 8, 9, 10):
                            f_rot(f, (h - 7) // 2, (h - 7) % 2)
                        if h == 14:
                            f_resid_k(f)
                        if h == 16:
                            f_low_k(f)
                    if has_early:
                        if h == 13:
                            f_stats0(b + 2, p)
                        if h == 20:
                            f_z1(b + 2)
                        if h == 29:
                            f_x1(b + 2, p)
                        if h == 31:
                            f_vy(b + 2)
                            f_rs2(b + 2)

            def tail():
                o_norm(last, 3)
                t_h(last, last % 2)
                norm(n2, h, t_negm[:, 0], t_rs[:, 0], h_negm, h_rstd, n2_ready, last + 1)
                t_n2T(last)
                for c in range(3):
                    t_up(last, c, LAST_BANKS[c])
                t_z2(last - 1)
                for c in range(3):
                    t_gate(last, c, LAST_BANKS[3 + c])
                t_x3(last - 1)
                t_x2(last)
                norm(n3, x2, t_negm[:, 1], t_rs[:, 1], x2_negm, x2_rstd, n3_ready, last + 1)
                t_z2(last)
                t_x3(last)

            batches(dve, first, body, tail)

        @block.tensor
        def _(pe):
            mm = nc.tensor.matmul
            pe.wait_ge(masks_made, 4)

            def transposes(dst, src, done):
                for t in range(TILES):
                    ins = nc.tensor.transpose(dst[:, t * P:(t + 1) * P], src[:, t, :], ident[:, :])
                ins.then_inc(done, 1)

            def spectral(dst, srcT, half, done):
                for i in range(2):
                    t = 2 * half + i
                    ins = mm(dst[:, i * 2 * P:(i + 1) * 2 * P], srcT[:, t * P:(t + 1) * P], spec_w[:, :],
                             start=True, stop=True)
                ins.then_inc(done, 1)

            def f_T0(f):
                pe.wait_ge(n0_ready, f + 1)
                if not (isinstance(f, int) and f < 1):
                    pe.wait_ge(front_read, 6 * f)
                transposes(f_ps, n0, early_mm)

            def f_spec(f, half, bank=None):
                pe.wait_ge(early_act, 3 * f + 1 + (half if bank is None else 0))
                spectral(f_ps if bank is None else bank, n0T, half, early_mm)

            def f_T1(f):
                pe.wait_ge(yn_ready, f + 1)
                pe.wait_ge(early_act, 3 * f + 3)
                transposes(f_ps, yn, front_mm)

            def f_proj(f, i, bank=None):
                pe.wait_ge(front_read, 6 * f + 1 + (i if bank is None else 0))
                mm(f_ps[:, :] if bank is None else bank, wqk[:, i, :], n1T[:, :], start=True, stop=True).then_inc(front_mm, 1)

            def f_v(f):
                pe.wait_ge(front_read, 6 * f + 5)
                for t in range(TILES):
                    ins = mm(f_ps[:, t * P:(t + 1) * P], n1T[:, t * P:(t + 1) * P], wv_sb[:, :], start=True, stop=True)
                ins.then_inc(front_mm, 1)

            def amax(a, p, c, j):
                quad = 4 * a + c
                if c == 0 and j == 0:
                    pe.wait_ge(k_stacked, K_DMAS * (a + 1))
                    pe.wait_ge(q_stacked, Q_DMAS * (a + 1))
                first_ever = isinstance(a, int) and a == 0 and c == 0
                if j >= 2 or (j == 0 and not first_ever):
                    pe.wait_ge(max_done, A_USES * quad + max(j - 1, 0))
                if j == 1 and not first_ever:
                    pe.wait_ge(maxT_out, quad)
                bank = a_ps[:, j % 2, :]
                if j == 0:
                    mm(bank, ident_b[:, :], causal_mask[:].rearrange("p h n -> p (h n)"), start=True, stop=True)
                    for hh in range(4):
                        pr, g = 2 * c + hh // 2, hh % 2
                        ins = mm(bank[:, hh * P:(hh + 1) * P], qz[0:SPLIT_ROWS, p, pr, g, 0:P],
                                 ks[0:SPLIT_ROWS, p, pr, 0:P], start=False, stop=True, skip_group_check=True)
                else:
                    t, pr = (j + 1) // 2, 2 * c + (j + 1) % 2
                    mm(bank, ident_b[:, :], band_mask[:].rearrange("p h n -> p (h n)"), start=True, stop=True)
                    for g in range(2):
                        ins = mm(bank[:, g * 2 * P:(g + 1) * 2 * P], qz[0:SPLIT_ROWS, p, pr, g, t * P:(t + 1) * P],
                                 ks[0:SPLIT_ROWS, p, pr, (t - 1) * P:(t + 1) * P], start=False, stop=True,
                                 skip_group_check=True)
                ins.then_inc(max_scores, 1)

            def maxT(a, c):
                pe.wait_ge(max_done, A_USES * (4 * a + c + 1))
                nc.tensor.transpose(a_ps[0:16, 1, 0:P], mx[:, c % 2, :, :, :].rearrange("p s g t -> p (s g t)"),
                                    ident[:, :]).then_inc(maxT_mm, 1)

            def score(b, p, v):
                c, kt, pr = v // 8, (v % 8) // 2, 2 * (v // 8) + v % 2
                if v % 8 == 0:
                    pe.wait_ge(shift_in, 16 * (4 * b + c + 1))
                if not (isinstance(b, int) and 32 * b + v < 3):
                    pe.wait_ge(exp_done, 32 * b + (v - 2 if v > 1 else v - 1))
                n = 2 * P if kt < 3 else P
                mm(s_ps[:, v % 3, 0:2 * n], ks[0:SHIFT_ROWS, p, pr, kt * P:(kt + 1) * P],
                   qz[0:SHIFT_ROWS, p, pr, :, kt * P:kt * P + n], start=True, stop=True).then_inc(scores, 1)

            def pv(b, p, s):
                c, kt = divmod(s, 4)
                pe.wait_ge(masked, 16 * b + s + 1)
                if kt == 0 and not (isinstance(b, int) and 4 * b + c < 1):
                    pe.wait_ge(attn_done, 4 * b + c)
                n = 2 * P if kt < 3 else P
                for hh in range(4):
                    ins = mm(o_ps[32 * hh:32 * hh + 32, kt * P:kt * P + n], vaug[:, p, kt, 4 * c + hh, :],
                             prob[:, s % 4, hh // 2, hh % 2, 0:n], start=(kt == 0), stop=(kt == 3),
                             skip_group_check=True)
                ins.then_inc(pv_done, 1)

            def oT(b, c):
                pe.wait_ge(o_out, 4 * b + c + 1)
                for t in range(TILES):
                    ins = nc.tensor.transpose(o_ps[:, t * P:(t + 1) * P], o_sb[:, t * P:(t + 1) * P], ident[:, :])
                ins.then_inc(oT_mm, 1)

            def t_attn(w):
                pe.wait_ge(attn_done, 4 * w + 4)
                if not (isinstance(w, int) and w < 1):
                    pe.wait_ge(tail_read, 10 * w)
                transposes(t_ps, attn, tail_mm)

            def t_wo(w):
                pe.wait_ge(tail_read, 10 * w + 1)
                for t in range(TILES):
                    ins = mm(t_ps[:, t * P:(t + 1) * P], attnT[:, t * P:(t + 1) * P], wo_sb[:, :], start=True, stop=True)
                ins.then_inc(tail_mm, 1)

            def t_n2(w):
                pe.wait_ge(n2_ready, w + 1)
                if isinstance(w, int) and w < 1:
                    pe.wait_ge(tail_read, 2)
                else:
                    pe.wait_ge(late_act, 3 * w)
                transposes(t_ps, n2, tail_mm)

            def t_ffn(w, i, bank=None):
                at, r = CHUNKS[i % 3]
                pe.wait_ge(tail_read, 10 * w + 3 + (i if bank is None else 0))
                mm((t_ps if bank is None else bank)[0:r, :], (w3_sb if i >= 3 else w1_sb)[:, at:at + r], n2T[:, :], start=True, stop=True).then_inc(tail_mm, 1)

            def t_w2(w, c, gates=9):
                pe.wait_ge(tail_read, 10 * w + gates)
                r = CHUNKS[c][1]
                for t in range(TILES):
                    ins = mm(t_ps[:, t * P:(t + 1) * P], gated[0:r, c, t * P:(t + 1) * P], w2_sb[0:r, c, :],
                             start=(c == 0 and t == 0), stop=(c == 2), skip_group_check=True)
                if c == 2:
                    ins.then_inc(tail_mm, 1)

            def t_n3(w):
                pe.wait_ge(n3_ready, w + 1)
                if isinstance(w, int) and w >= last - 1:
                    pe.wait_ge(tail_read, 10 * last + (10 if w == last else 2))
                else:
                    pe.wait_ge(tail_read, 10 * w + 12)
                transposes(t_ps, n3, late_mm)

            def t_spec(w, half, bank=None):
                pe.wait_ge(late_act, 3 * w + 1 + (half if bank is None else 0))
                spectral(t_ps if bank is None else bank, n3T, half, late_mm)

            def first():
                for f in range(2):
                    f_T0(f)
                    if f == 0:
                        pe.wait_ge(spec_ready, 2)
                    f_spec(f, 0, SPEC_BANKS[0])
                    f_spec(f, 1, SPEC_BANKS[1])
                    if f == 0:
                        f_T1(0)
                        pe.wait_ge(rot_ready, 4)
                        for i in range(4):
                            f_proj(0, i, FIRST_BANKS[i])
                        f_v(0)
                pe.wait_ge(early_act, 6)
                for j in range(A_USES):
                    amax(0, 0, 0, j)
                maxT(0, 0)
                pe.wait_ge(ones_made, 2)
                pe.wait_ge(tail_in, 16 * 5)

            def body(b, p, has_early, has_front, has_tail, has_late):
                f, w = b + 1, b - 1
                for h in range(UNITS):
                    c, k = divmod(h, 8)
                    uses = MAX_AT[k] if c < 3 or has_front else ()
                    a = (b, p, c + 1) if c < 3 else (f, 1 - p, 0)
                    score(b, p, h)
                    if h == 1 and has_tail:
                        pv(w, 1 - p, 15)
                    for j in uses[0:1]:
                        amax(*a, j)
                    if h == 3 and has_tail:
                        oT(w, 3)
                    if h in (11, 19, 27):
                        oT(b, h // 8 - 1)
                    if has_tail:
                        if h == 10:
                            t_n2(w)
                        if h in (11, 12, 13):
                            t_ffn(w, h - 11)
                        if h == 20:
                            t_w2(w, 0)
                            t_w2(w, 1)
                        if h == 21:
                            t_w2(w, 2)
                    if has_late:
                        if h == 7:
                            t_n3(b - 2)
                        if h in (8, 9):
                            t_spec(b - 2, h - 8)
                    for j in uses[1:]:
                        amax(*a, j)
                    if has_tail:
                        if h == 4:
                            t_attn(w)
                        if h == 5:
                            t_wo(w)
                    if has_tail and h in (14, 16, 18):
                        t_ffn(w, 3 + (h - 14) // 2)
                    if has_front:
                        if h == 3:
                            f_T1(f)
                        if h in (7, 8, 9, 10):
                            f_proj(f, h - 7)
                        if h == 11:
                            f_v(f)
                    if has_early:
                        if h == 18:
                            f_T0(b + 2)
                        if h in (19, 20):
                            f_spec(b + 2, h - 19)
                    if k == MAXT_AT and (c < 3 or has_front):
                        maxT(a[0], a[2])
                    if h % 2 == 1 and h >= 5:
                        s = (h - 3) // 2
                        if s % 4 == 1:
                            pv(b, p, s - 1)
                        if s % 4 != 0:
                            pv(b, p, s)

            def tail():
                w, p = last, last % 2
                pv(w, p, 15)
                oT(w, 3)
                t_attn(w)
                t_wo(w)
                t_n3(w - 1)
                t_spec(w - 1, 0, SPEC_BANKS[0])
                t_spec(w - 1, 1, SPEC_BANKS[1])
                t_n2(w)
                for i in range(6):
                    t_ffn(w, i, LAST_BANKS[i])
                for c in range(3):
                    t_w2(w, c, 7 + c)
                t_n3(w)
                t_spec(w, 0, SPEC_BANKS[0])
                t_spec(w, 1, SPEC_BANKS[1])

            batches(pe, first, body, tail)


_INS = ['L0_attn_x', 'L0_attn_wq', 'L0_attn_wk', 'L0_attn_wv', 'L0_attn_wo', 'L0_attn_w1', 'L0_attn_w2', 'L0_attn_w3',
        'L0_attn_ln1_g', 'L0_attn_ln1_b', 'L0_attn_ln2_g', 'L0_attn_ln2_b', 'L0_ffn_theta', 'L0_ffn_phi',
        'L0_ffn_theta_noise', 'L0_ffn_phi_noise']


def rope_tables():
    freqs = (1.0 / np.float32(THETA) ** (np.arange(0, HD, 2, dtype=np.float32) / np.float32(HD))).astype(np.float32)
    angle = np.outer(freqs, np.arange(SEQ, dtype=np.float32)).astype(np.float32)
    rows = np.tile(np.repeat(angle, 2, axis=0), (HEADS, 1))
    return np.cos(rows).astype(np.float32), np.sin(rows).astype(np.float32)


def kernel(**inputs):
    import concourse.bacc as bacc
    from concourse.bass_utils import run_bass_kernel_spmd as run

    nc = bacc.Bacc("TRN2", target_bir_lowering=False, num_devices=1)
    arrays, aps = {}, {}

    def give(name, a):
        arrays[name] = a
        aps[name] = nc.dram_tensor(name, a.shape, mybir.dt.from_np(a.dtype), kind="ExternalInput").ap()

    for name in _INS:
        a = np.ascontiguousarray(inputs[name])
        give(name, a.reshape(DIM, 1) if a.ndim == 1 else a)
    cos_t, sin_t = rope_tables()
    give("cos_table", cos_t)
    give("sin_table", sin_t)
    out = nc.dram_tensor("out", (BATCH, SEQ, DIM), FP32, kind="ExternalOutput").ap()
    a = {n.replace("L0_attn_", "").replace("L0_ffn_", ""): v for n, v in aps.items()}
    build(nc, a["x"], a["cos_table"], a["sin_table"], a["wq"], a["wk"], a["wv"], a["wo"], a["w1"], a["w2"], a["w3"],
          a["ln1_g"], a["ln1_b"], a["ln2_g"], a["ln2_b"], a["theta"], a["phi"], a["theta_noise"], a["phi_noise"], out)
    r = run(nc, [arrays], core_ids=[0])
    return r.results[0]["out"]
```

```python
import math

import concourse.bass as bass
import concourse.mybir as mybir
import numpy as np
from contextlib import ExitStack

FP32 = mybir.dt.float32
BF16 = mybir.dt.bfloat16
ALU = mybir.AluOpType
ACT = mybir.ActivationFunctionType
AX = mybir.AxisListType.X

BATCH, SEQ, DIM = 8, 512, 128
HEADS = 16
HD = DIM // HEADS
HIDDEN = 352
P = 128
TILES = SEQ // P
PAIRS = HEADS // 2
QUADS = HEADS // 4
CHUNKS = [(0, 128), (128, 128), (256, 96)]
EPS = 1e-5
TINY = 1e-19
THETA = 10000.0
SCALE = HD ** -0.5
NEG = -1e30
SLOTS_Q = (0, 0, 0, 1, 1, 2)
SLOTS_K = (0, 1, 2, 0, 1, 0)
SPLIT_ROWS = 16 * len(SLOTS_Q)
SHIFT_ROWS = SPLIT_ROWS + 1
K_DMAS, Q_DMAS = 16 * 3, 16 * 12
A_USES = 7
MAX_AT = ((0, 1), (), (2, 3), (4,), (5, 6), (), (), ())
UNITS = 2 * 4 * QUADS

PLACE = dict(
    pool_yn=1, pool_n3=3, pool_n2=7, pool_rope_q=8, pool_resid_q=10, pool_rope_k=12, pool_low_q=12,
    pool_gate=(14, 16, 18), pool_n0=15, pool_y=18, pool_xy=23,
    act_o=2, act_n1T=4, act_attnT=4, act_maxT=5, act_rstd2=7, act_n3T=7, act_square3=(7, 9), act_high_q=9,
    act_mid_q=10, act_v=11, act_high_k=12, act_exp_u=(12, 14, 16), act_ln_u=(12, 14, 16), act_silu=(13, 15, 17),
    act_rstd0=14, act_mid_k=16, act_mag3=19, act_n0T=22, act_square0=(23, 24), act_rstd3=26, act_mag0=26,
    act_rstd1=30, act_rstd1b=31,
    dve_o=3, dve_rot=(7, 8, 9, 10), dve_h=7, dve_stats2=7, dve_moments2=7, dve_n2T=10, dve_up=(11, 12, 15),
    dve_stats0=13, dve_moments0=13, dve_resid_k=14, dve_low_k=16, dve_gate=(16, 18, 19), dve_z3=16, dve_x3=20,
    dve_x2=23, dve_stats3=23, dve_z0=25, dve_moments3=25, dve_x1=29, dve_stats1=30, dve_rstd1=31,
    dve_moments1=31,
    pe_oT=3, pe_T1=4, pe_attn=4, pe_maxT=5, pe_wo=5, pe_proj=(7, 8, 9, 10), pe_T3=7, pe_spec3=(8, 9), pe_T2=10,
    pe_v=11, pe_up=(11, 12, 13), pe_gate=(14, 16, 18), pe_w2=(21, 21, 21), pe_T0=22, pe_spec0=(23, 24),
)


def build(nc, x, cos_t, sin_t, wq, wk, wv, wo, w1, w2, w3, g1, b1, g2, b2,
          theta, phi, theta_n, phi_n, out):
    ctx = ExitStack()
    with ctx:
        def sb(name, shape, dt=FP32):
            return ctx.enter_context(nc.sbuf_tensor(name, shape, dt))

        def sem(name):
            return ctx.enter_context(nc.semaphore(name))

        ident = sb("ident", [P, P])
        ident_b = sb("ident_b", [P, P], BF16)
        band_mask = sb("band_mask", [P, 2, 2 * P], BF16)
        causal_mask = sb("causal_mask", [P, 4, P], BF16)
        cos_sb = sb("cos_sb", [P, SEQ])
        sin_sb = sb("sin_sb", [P, SEQ])
        wqk = sb("wqk", [P, 4, P])
        wv_sb = sb("wv_sb", [P, P])
        wo_sb = sb("wo_sb", [P, P])
        w1_sb = sb("w1_sb", [P, HIDDEN])
        w3_sb = sb("w3_sb", [P, HIDDEN])
        w2_sb = sb("w2_sb", [P, 3, P])
        gb = sb("gb", [P, 4])
        raw = sb("raw", [P, 4, P])
        ang = sb("ang", [P, 2, P])
        turns = sb("turns", [P, 2, P])
        spec_w = sb("spec_w", [P, 2 * P])

        xt = sb("xt", [P, 2, TILES, P])
        f_st = sb("f_st", [P, 2, TILES, 6])
        f_mv = sb("f_mv", [P, 2, TILES, 2])
        f_negm = sb("f_negm", [P, 2, TILES])
        f_ln = sb("f_ln", [P, 3, TILES])
        f_rs = sb("f_rs", [P, 4, TILES])
        f_vyt = sb("f_vyt", [P, 2, TILES])
        eps_ap = sb("eps_ap", [P, 4])
        n0 = sb("n0", [P, TILES, P])
        n0T = sb("n0T", [P, SEQ])
        f_sq = sb("f_sq", [P, TILES, 2 * P])
        f_z = sb("f_z", [P, TILES, P])
        x1 = sb("x1", [P, TILES, P])
        y = sb("y", [P, 2, TILES, P])
        xy = sb("xy", [P, 2, TILES, P])
        yn = sb("yn", [P, TILES, P])
        n1T = sb("n1T", [P, SEQ])
        rot = sb("rot", [P, 2, 2, SEQ])
        roped = sb("roped", [P, 2, SEQ])
        resid = sb("resid", [P, 2, SEQ])
        parts = sb("parts", [P, 2, 3, SEQ], BF16)
        vaug = sb("vaug", [P, 2, TILES, HEADS, 32])
        qz = sb("qz", [P, 2, PAIRS, 2, SEQ], BF16)
        ks = sb("ks", [P, 2, PAIRS, SEQ], BF16)

        mx = sb("mx", [P, 2, 2, 2, TILES])
        mxT = sb("mxT", [16, 2, P], BF16)
        prob = sb("prob", [P, 4, 2, 2, 2 * P])
        o_sb = sb("o_sb", [P, SEQ])
        rden = sb("rden", [P, TILES, 4])
        attn = sb("attn", [P, TILES, P])

        t_st = sb("t_st", [P, 2, TILES, 6])
        t_mv = sb("t_mv", [P, 2, TILES, 2])
        t_negm = sb("t_negm", [P, 2, TILES])
        t_ln = sb("t_ln", [P, 2, TILES])
        t_rs = sb("t_rs", [P, 2, TILES])
        attnT = sb("attnT", [P, SEQ])
        h = sb("h", [P, TILES, P])
        hx1 = sb("hx1", [P, TILES, P])
        n2 = sb("n2", [P, TILES, P])
        n2T = sb("n2T", [P, SEQ])
        up = sb("up", [P, 3, SEQ])
        sg = sb("sg", [P, 3, SEQ])
        act_up = sb("act_up", [P, 3, SEQ])
        gated = sb("gated", [P, 3, SEQ])
        x2 = sb("x2", [P, TILES, P])
        n3 = sb("n3", [P, TILES, P])
        n3T = sb("n3T", [P, SEQ])
        t_sq = sb("t_sq", [P, TILES, 2 * P])
        t_z = sb("t_z", [P, TILES, P])
        x3 = sb("x3", [P, TILES, P])

        s_ps = ctx.enter_context(nc.psum_tensor("s_ps", [P, 3, 512], FP32))
        a_ps = ctx.enter_context(nc.psum_tensor("a_ps", [P, 2, 512], FP32))
        o_ps = ctx.enter_context(nc.psum_tensor("o_ps", [P, 512], FP32))
        f_ps = ctx.enter_context(nc.psum_tensor("f_ps", [P, 512], FP32))
        t_ps = ctx.enter_context(nc.psum_tensor("t_ps", [P, 512], FP32))

        angles_in = sem("angles_in")
        qk_in = sem("qk_in")
        front_in = sem("front_in")
        tail_in = sem("tail_in")
        consts_made = sem("consts_made")
        masks_made = sem("masks_made")
        ones_made = sem("ones_made")
        consts_dve = sem("consts_dve")
        angles = sem("angles")
        angle_step = sem("angle_step")
        spec_ready = sem("spec_ready")
        rot_ready = sem("rot_ready")
        x_in = sem("x_in")
        x_stats = sem("x_stats")
        x_mv = sem("x_mv")
        x_negm = sem("x_negm")
        x_lnvar = sem("x_lnvar")
        x_rstd = sem("x_rstd")
        n0_ready = sem("n0_ready")
        early_mm = sem("early_mm")
        early_act = sem("early_act")
        front_mm = sem("front_mm")
        front_read = sem("front_read")
        z1_ready = sem("z1_ready")
        lnz1 = sem("lnz1")
        mag1 = sem("mag1")
        x1_ready = sem("x1_ready")
        x1_stats = sem("x1_stats")
        x1_mv = sem("x1_mv")
        x1_negm = sem("x1_negm")
        x1_lnvar = sem("x1_lnvar")
        x1_rstd = sem("x1_rstd")
        vy_part = sem("vy_part")
        vy_ready = sem("vy_ready")
        vy_ln = sem("vy_ln")
        vy_rstd = sem("vy_rstd")
        rs2_ready = sem("rs2_ready")
        y_ready = sem("y_ready")
        xy_ready = sem("xy_ready")
        yn_ready = sem("yn_ready")
        roped_ready = sem("roped_ready")
        high_ready = sem("high_ready")
        resid_q = sem("resid_q")
        resid_k = sem("resid_k")
        mid_ready = sem("mid_ready")
        low_q = sem("low_q")
        low_k = sem("low_k")
        q_spilled = sem("q_spilled")
        k_spilled = sem("k_spilled")
        k_stacked = sem("k_stacked")
        q_stacked = sem("q_stacked")
        max_scores = sem("max_scores")
        max_done = sem("max_done")
        maxT_mm = sem("maxT_mm")
        maxT_out = sem("maxT_out")
        shift_in = sem("shift_in")
        scores = sem("scores")
        exp_done = sem("exp_done")
        masked = sem("masked")
        pv_done = sem("pv_done")
        o_out = sem("o_out")
        oT_mm = sem("oT_mm")
        den_done = sem("den_done")
        attn_done = sem("attn_done")
        tail_mm = sem("tail_mm")
        tail_read = sem("tail_read")
        late_mm = sem("late_mm")
        late_act = sem("late_act")
        h_stats = sem("h_stats")
        h_mv = sem("h_mv")
        h_negm = sem("h_negm")
        h_lnvar = sem("h_lnvar")
        h_rstd = sem("h_rstd")
        n2_ready = sem("n2_ready")
        silu_e = sem("silu_e")
        silu_l = sem("silu_l")
        silu_s = sem("silu_s")
        silu_u = sem("silu_u")
        x2_stats = sem("x2_stats")
        x2_mv = sem("x2_mv")
        x2_negm = sem("x2_negm")
        x2_lnvar = sem("x2_lnvar")
        x2_rstd = sem("x2_rstd")
        n3_ready = sem("n3_ready")
        z2_ready = sem("z2_ready")
        lnz2 = sem("lnz2")
        mag2 = sem("mag2")
        x3_ready = sem("x3_ready")
        stored = sem("stored")
        waits_passed = sem("waits_passed")

        q_dram = nc.dram_tensor("q_dram", (3, P, SEQ), BF16).ap()
        k_dram = nc.dram_tensor("k_dram", (PAIRS, 3, 16, SEQ), BF16).ap()

        SPEC_BANKS = (a_ps[:, 0, :], a_ps[:, 1, :])
        FIRST_BANKS = (f_ps[:, :], s_ps[:, 0, :], s_ps[:, 1, :], s_ps[:, 2, :])
        FFN_BANKS = (t_ps[:, :], f_ps[:, :]) * 3
        LAST_BANKS = (s_ps[:, 0, :], s_ps[:, 1, :], s_ps[:, 2, :], a_ps[:, 0, :], a_ps[:, 1, :], f_ps[:, :])

        block = ctx.enter_context(nc.Block())
        last = BATCH - 1

        def wait_alone(eng, s, n):
            eng.wait_ge(s, n)
            eng.sem_inc(waits_passed, 1)

        def batches(eng, first, body, tail):
            def peeled(b):
                body(b, b % 2, b + 2 <= last, b + 1 <= last, b >= 1, b >= 2)

            first()
            peeled(0)
            peeled(1)
            with eng.Fori(1, BATCH // 2 - 1) as pair:
                body(2 * pair, 0, True, True, True, True)
                body(2 * pair + 1, 1, True, True, True, True)
            peeled(last - 1)
            peeled(last)
            tail()

        @block.sync
        def _(sp):
            loads = (
                (angles_in, raw[:, 0, :], theta), (angles_in, raw[:, 1, :], theta_n),
                (angles_in, raw[:, 2, :], phi), (angles_in, raw[:, 3, :], phi_n),
                (qk_in, wqk[:, 0, :], wq), (qk_in, wqk[:, 2, :], wk),
                (front_in, gb[:, 0:1], g1), (front_in, gb[:, 1:2], b1),
                (front_in, gb[:, 2:3], g2), (front_in, gb[:, 3:4], b2),
                (front_in, cos_sb[:, :], cos_t), (front_in, sin_sb[:, :], sin_t), (front_in, wv_sb[:, :], wv),
                (tail_in, wo_sb[:, :], wo), (tail_in, w1_sb[:, :], w1), (tail_in, w3_sb[:, :], w3),
                (tail_in, w2_sb[:, 0:2, :], w2[0:256, :].rearrange("(c p) d -> p c d", p=P)),
                (tail_in, w2_sb[0:96, 2, :], w2[256:352, :]),
            )

            sp.sem_inc(stored, 16)

            def load_x(f, p):
                if not (isinstance(f, int) and f < 2):
                    wait_alone(sp, x1_ready, f - 1)
                if not (isinstance(f, int) and f < 1):
                    wait_alone(sp, x_in, 16 * f)
                sp.dma_start(xt[:, p, :, :], x[f].rearrange("(t p) d -> p t d", p=P)).then_inc(x_in, 16)

            def stack(f, p):
                if not (isinstance(f, int) and f < 1):
                    wait_alone(sp, q_stacked, Q_DMAS * f)
                    wait_alone(sp, k_stacked, K_DMAS * f)
                def spill_q(part, s, n):
                    sp.wait_ge(s, n)
                    sp.dma_start(q_dram[part], parts[:, 0, part, :]).then_inc(q_spilled, 16)

                def spill_k(part, s, n):
                    sp.wait_ge(s, n)
                    sp.dma_start(k_dram[:, part], parts[:, 1, part, :]).then_inc(k_spilled, 16)

                def stack_q(part):
                    wait_alone(sp, q_spilled, 48 * f + 16 * (part + 1))
                    if part == 0 and not (isinstance(f, int) and f < 2):
                        sp.wait_ge(pv_done, 16 * (f - 1))
                    src = q_dram[part].rearrange("(s g d) n -> g d s n", g=2, d=HD)
                    for j in range(len(SLOTS_Q)):
                        for g in range(2) if SLOTS_Q[j] == part else ():
                            sp.dma_start(qz[16 * j + 8 * g:16 * j + 8 * g + 8, p, :, g, :], src[g]).then_inc(q_stacked, 16)

                spill_q(0, high_ready, 2 * f + 1)
                stack_q(0)
                spill_q(1, mid_ready, 2 * f + 1)
                spill_k(0, high_ready, 2 * f + 2)
                stack_q(1)
                spill_q(2, low_q, f + 1)
                spill_k(1, mid_ready, 2 * f + 2)
                spill_k(2, low_k, f + 1)
                stack_q(2)
                sp.wait_ge(k_spilled, 48 * (f + 1))
                for row, n in ((0, 3), (48, 2), (80, 1)):
                    sp.dma_start(ks[row:row + 16 * n, p, :, :],
                                 k_dram[:, 0:n].rearrange("s a r n -> (a r) s n")).then_inc(k_stacked, 16)

            def store(w):
                wait_alone(sp, x3_ready, w + 1)
                sp.dma_start(out[w].rearrange("(t p) d -> p t d", p=P), x3[:, :, :]).then_inc(stored, 16)

            def step(f, p):
                if not (isinstance(f, int) and f == last):
                    load_x(f + 1, 1 - p)
                stack(f, p)
                if not (isinstance(f, int) and f < 3):
                    store(f - 3)

            load_x(0, 0)
            for done, dst, src in loads:
                sp.dma_start(dst, src).then_inc(done, 16)
            wait_alone(sp, consts_dve, 5)
            wait_alone(sp, ones_made, 2)
            for f in range(3):
                step(f, f % 2)
            with sp.Fori(1, BATCH // 2 - 1) as pair:
                step(2 * pair + 1, 1)
                step(2 * pair + 2, 0)
            step(last, 1)
            for w in range(BATCH - 3, BATCH):
                store(w)
            sp.wait_ge(stored, 16 * BATCH + 16)

        @block.gpsimd
        def _(pool):
            for n, (t, v) in enumerate(((ident, 0.0), (ident_b, 0.0), (band_mask, 0.0), (causal_mask, 0.0))):
                nc.gpsimd.memset(t[:], v).then_inc(consts_made, 1)
            pool.wait_ge(consts_made, 4)
            for t in (ident, ident_b):
                nc.gpsimd.affine_select(out=t[:, :], in_=t[:, :], compare_op=ALU.not_equal, fill=1.0, base=0,
                                        pattern=[[-1, P]], channel_multiplier=1).then_inc(masks_made, 1)
            nc.gpsimd.affine_select(out=causal_mask[:], in_=causal_mask[:], compare_op=ALU.is_ge, fill=NEG, base=0,
                                    pattern=[[0, 4], [-1, P]], channel_multiplier=1).then_inc(masks_made, 1)
            nc.gpsimd.affine_select(out=band_mask[:], in_=band_mask[:], compare_op=ALU.is_ge, fill=NEG, base=0,
                                    pattern=[[0, 2], [1, 2 * P]], channel_multiplier=-1).then_inc(consts_made, 1)
            pool.wait_ge(consts_made, 5)
            nc.gpsimd.affine_select(out=band_mask[:], in_=band_mask[:], compare_op=ALU.is_ge, fill=NEG, base=P,
                                    pattern=[[0, 2], [-1, 2 * P]], channel_multiplier=1).then_inc(masks_made, 1)

            def ones():
                nc.gpsimd.memset(ks[:], 1.0).then_inc(ones_made, 1)
                nc.gpsimd.memset(vaug[:], 1.0).then_inc(ones_made, 1)

            def norm(dst, src, negm, rs, done):
                for t in range(TILES):
                    ins = nc.gpsimd.tensor_scalar(dst[:, t, :], src[:, t, :], negm[:, t:t + 1], rs[:, t:t + 1],
                                                  ALU.add, ALU.mult)
                ins.then_inc(done, 1)

            def f_n0(f, p):
                pool.wait_ge(x_rstd, f + 1)
                wait_alone(pool, x_negm, f + 1)
                norm(n0, xt[:, p], f_negm[:, 0], f_rs[:, 0], n0_ready)

            def f_yn(f):
                pool.wait_ge(rs2_ready, f + 1)
                wait_alone(pool, x1_negm, f + 1)
                norm(yn, x1, f_negm[:, 1], f_rs[:, 3], yn_ready)

            def f_y(f, p):
                norm(y[:, p], x1, f_negm[:, 1], f_rs[:, 1], y_ready)

            def f_xy(f, p):
                pool.wait_ge(y_ready, f + 1)
                nc.gpsimd.tensor_tensor(xy[:, p, :, :], x1[:, :, :], y[:, p, :, :], ALU.add).then_inc(xy_ready, 1)

            def f_rope(f, i):
                pool.wait_ge(front_read, 6 * f + 3 + 2 * i)
                nc.gpsimd.tensor_tensor(roped[:, i, :], rot[:, i, 0, :], rot[:, i, 1, :], ALU.add).then_inc(roped_ready, 1)

            def f_resid_q(f):
                pool.wait_ge(high_ready, 2 * f + 1)
                nc.gpsimd.tensor_tensor(resid[:, 0, :], roped[:, 0, :], parts[:, 0, 0, :], ALU.subtract).then_inc(resid_q, 1)

            def f_low_q(f):
                pool.wait_ge(mid_ready, 2 * f + 1)
                pool.wait_ge(resid_q, f + 1)
                nc.gpsimd.tensor_tensor(parts[:, 0, 2, :], resid[:, 0, :], parts[:, 0, 1, :], ALU.subtract).then_inc(low_q, 1)

            def mask(b, s):
                kt = s % 4
                wait_alone(pool, exp_done, 32 * b + 2 * s + 2)
                own = prob[:, s % 4, :, :, 0:P].rearrange("p a g n -> p (a g) n")
                ins = nc.gpsimd.affine_select(out=own, in_=own, compare_op=ALU.is_ge, fill=0.0, base=0,
                                              pattern=[[0, 4], [1, P]], channel_multiplier=-1)
                if kt < 3:
                    nxt = prob[:, s % 4, :, :, P:2 * P].rearrange("p a g n -> p (a g) n")
                    ins = nc.gpsimd.affine_select(out=nxt, in_=nxt, compare_op=ALU.is_ge, fill=0.0, base=0,
                                                  pattern=[[0, 4], [-1, P]], channel_multiplier=1)
                ins.then_inc(masked, 1)

            def t_n2(w):
                pool.wait_ge(h_rstd, w + 1)
                wait_alone(pool, h_negm, w + 1)
                norm(n2, h, t_negm[:, 0], t_rs[:, 0], n2_ready)

            def t_u(w, c):
                pool.wait_ge(silu_s, 3 * w + c + 1)
                r = CHUNKS[c][1]
                nc.gpsimd.tensor_tensor(act_up[0:r, c, :], up[0:r, c, :], sg[0:r, c, :], ALU.mult).then_inc(silu_u, 1)

            def t_n3(w):
                pool.wait_ge(x2_rstd, w + 1)
                wait_alone(pool, x2_negm, w + 1)
                norm(n3, x2, t_negm[:, 1], t_rs[:, 1], n3_ready)

            def first():
                ones()
                f_rope(0, 0)
                f_resid_q(0)
                f_rope(0, 1)
                f_low_q(0)
                wait_alone(pool, x1_negm, 1)
                f_y(0, 0)
                f_xy(0, 0)
                f_n0(1, 1)

            def body(b, p, has_early, has_front, has_tail, has_late):
                at, f, w = PLACE, b + 1, b - 1
                for h in range(UNITS):
                    if h % 2 == 1:
                        mask(b, h // 2)
                    if has_tail:
                        if h == at["pool_n2"]:
                            t_n2(w)
                        for c in range(3):
                            if h == at["pool_gate"][c]:
                                t_u(w, c)
                    if has_early and h == at["pool_n0"]:
                        f_n0(b + 2, p)
                    if has_late and h == at["pool_n3"]:
                        t_n3(b - 2)
                    if has_front:
                        if h == at["pool_yn"]:
                            f_yn(f)
                        if h == at["pool_rope_q"]:
                            f_rope(f, 0)
                        if h == at["pool_resid_q"]:
                            f_resid_q(f)
                        if h == at["pool_rope_k"]:
                            f_rope(f, 1)
                        if h == at["pool_low_q"]:
                            f_low_q(f)
                        if h == at["pool_y"]:
                            f_y(f, 1 - p)
                        if h == at["pool_xy"]:
                            f_xy(f, 1 - p)

            def tail():
                t_n3(last - 1)
                for c in range(3):
                    t_u(last, c)

            batches(pool, first, body, tail)

        @block.scalar
        def _(act):
            def spectral_weights():
                act.wait_ge(angles, 6)
                nc.scalar.activation(spec_w[:, 0:P], ang[:, 0, :], ACT.Sin).then_inc(spec_ready, 1)
                nc.scalar.activation(spec_w[:, P:2 * P], ang[:, 1, :], ACT.Sin).then_inc(spec_ready, 1)

            def rsqrt(dst, tmp, var, lnsem, done, n):
                nc.scalar.activation(tmp, var, ACT.Ln, bias=eps_ap[:, 0:1]).then_inc(lnsem, 1)
                act.wait_ge(lnsem, n)
                nc.scalar.activation(dst, tmp, ACT.Exp, scale=-0.5).then_inc(done, 1)

            def magnitude(dst, tmp, z, lnsem, done, n):
                nc.scalar.activation(tmp, z, ACT.Ln, bias=eps_ap[:, 1:2]).then_inc(lnsem, 1)
                act.wait_ge(lnsem, n)
                nc.scalar.activation(dst, tmp, ACT.Exp, scale=0.5, bias=eps_ap[:, 2:3]).then_inc(done, 1)

            def f_rs0(f):
                act.wait_ge(x_mv, f + 1)
                rsqrt(f_rs[:, 0, :], f_ln[:, 0, :], f_mv[:, 0, :, 1], x_lnvar, x_rstd, f + 1)

            def f_n0T(f):
                act.wait_ge(early_mm, 3 * f + 1)
                nc.scalar.activation(n0T[:, :], f_ps[:, :], ACT.Copy).then_inc(early_act, 1)

            def f_square(f, half, bank=None):
                act.wait_ge(early_mm, 3 * f + 2 + half)
                nc.scalar.activation(f_sq[:, 2 * half:2 * half + 2, :].rearrange("p t n -> p (t n)"),
                                     f_ps[:, :] if bank is None else bank, ACT.Square).then_inc(early_act, 1)

            def f_mag1(f):
                act.wait_ge(z1_ready, f + 1)
                magnitude(f_z[:, :, :], f_z[:, :, :], f_z[:, :, :], lnz1, mag1, f + 1)

            def f_rs1(f):
                act.wait_ge(x1_mv, f + 1)
                rsqrt(f_rs[:, 1, :], f_ln[:, 1, :], f_mv[:, 1, :, 1], x1_lnvar, x1_rstd, f + 1)

            def f_rs2(f):
                act.wait_ge(vy_ready, f + 1)
                rsqrt(f_rs[:, 2, :], f_ln[:, 2, :], f_vyt[:, 1, :], vy_ln, vy_rstd, f + 1)

            def f_n1T(f):
                act.wait_ge(front_mm, 6 * f + 1)
                nc.scalar.activation(n1T[:, :], f_ps[:, :], ACT.Identity, scale=gb[:, 0:1],
                                     bias=gb[:, 1:2]).then_inc(front_read, 1)

            def f_v(f, p):
                act.wait_ge(front_mm, 6 * f + 6)
                if not (isinstance(f, int) and f < 2):
                    act.wait_ge(pv_done, 16 * (f - 1))
                nc.scalar.activation(vaug[:, p, :, :, 0:HD].rearrange("p t h d -> p (t h) d"),
                                     f_ps[:, :].rearrange("p (a d) -> p a d", d=HD), ACT.Copy).then_inc(front_read, 1)

            def f_high(f, i):
                act.wait_ge(roped_ready, 2 * f + i + 1)
                if not (isinstance(f, int) and f < 1):
                    act.wait_ge(k_spilled if i else q_spilled, 48 * f)
                nc.scalar.activation(parts[:, i, 0, :], roped[:, i, :], ACT.Copy).then_inc(high_ready, 1)

            def f_mid(f, i):
                act.wait_ge(resid_k if i else resid_q, f + 1)
                nc.scalar.activation(parts[:, i, 1, :], resid[:, i, :], ACT.Copy).then_inc(mid_ready, 1)

            def maxT(a, c):
                act.wait_ge(maxT_mm, 4 * a + c + 1)
                if not (isinstance(a, int) and 4 * a + c < 2):
                    act.wait_ge(shift_in, 16 * (4 * a + c - 1))
                nc.scalar.activation(mxT[:, c % 2, :], a_ps[0:16, 1, 0:P], ACT.Copy, scale=-1.0).then_inc(maxT_out, 1)

            def shift(a, p, c):
                act.wait_ge(maxT_out, 4 * a + c + 1)
                dst = qz[SPLIT_ROWS:SHIFT_ROWS, p, 2 * c:2 * c + 2, :, :].rearrange("o s g n -> o (s g n)")
                act.dma_start(dst, mxT[:, c % 2, :]).then_inc(shift_in, 16)

            def exp(b, v):
                kt = (v % 8) // 2
                act.wait_ge(scores, 32 * b + v + 1)
                if not (isinstance(b, int) and 16 * b + v // 2 < 4):
                    act.wait_ge(pv_done, 16 * b + v // 2 - 3)
                n = 2 * P if kt < 3 else P
                bank = s_ps[:, v % 3, 0:2 * n].rearrange("p (g n) -> p g n", g=2)
                nc.scalar.activation(prob[:, (v // 2) % 4, v % 2, :, 0:n], bank, ACT.Exp, scale=SCALE).then_inc(exp_done, 1)

            def o_copy(b, c):
                act.wait_ge(pv_done, 16 * b + 4 * c + 4)
                nc.scalar.activation(o_sb[:, :], o_ps[:, :], ACT.Copy).then_inc(o_out, 1)

            def t_attnT(w):
                act.wait_ge(tail_mm, 10 * w + 1)
                nc.scalar.activation(attnT[:, :], t_ps[:, :], ACT.Copy).then_inc(tail_read, 1)

            def t_rs0(w):
                act.wait_ge(h_mv, w + 1)
                rsqrt(t_rs[:, 0, :], t_ln[:, 0, :], t_mv[:, 0, :, 1], h_lnvar, h_rstd, w + 1)

            def t_exp_u(w, c):
                r = CHUNKS[c][1]
                act.wait_ge(tail_read, 10 * w + 4 + c)
                nc.scalar.activation(sg[0:r, c, :], up[0:r, c, :], ACT.Exp, scale=-1.0).then_inc(silu_e, 1)

            def t_ln_u(w, c):
                r = CHUNKS[c][1]
                act.wait_ge(silu_e, 3 * w + c + 1)
                nc.scalar.activation(sg[0:r, c, :], sg[0:r, c, :], ACT.Ln, bias=eps_ap[0:r, 3:4]).then_inc(silu_l, 1)

            def t_sig(w, c):
                r = CHUNKS[c][1]
                act.wait_ge(silu_l, 3 * w + c + 1)
                nc.scalar.activation(sg[0:r, c, :], sg[0:r, c, :], ACT.Exp, scale=-1.0).then_inc(silu_s, 1)

            def t_rs1(w):
                act.wait_ge(x2_mv, w + 1)
                rsqrt(t_rs[:, 1, :], t_ln[:, 1, :], t_mv[:, 1, :, 1], x2_lnvar, x2_rstd, w + 1)

            def t_n3T(w):
                act.wait_ge(late_mm, 3 * w + 1)
                nc.scalar.activation(n3T[:, :], t_ps[:, :], ACT.Copy).then_inc(late_act, 1)

            def t_square(w, half, bank=None):
                act.wait_ge(late_mm, 3 * w + 2 + half)
                nc.scalar.activation(t_sq[:, 2 * half:2 * half + 2, :].rearrange("p t n -> p (t n)"),
                                     t_ps[:, :] if bank is None else bank, ACT.Square).then_inc(late_act, 1)

            def t_mag2(w):
                act.wait_ge(z2_ready, w + 1)
                magnitude(t_z[:, :, :], t_z[:, :, :], t_z[:, :, :], lnz2, mag2, w + 1)

            def first():
                for f in range(2):
                    if f == 0:
                        act.preload_act_table_set("natural_log_exp_and_others")
                    f_rs0(f)
                    if f == 0:
                        spectral_weights()
                        act.preload_act_table_set("natural_log_exp_and_others")
                    f_n0T(f)
                    f_square(f, 0, SPEC_BANKS[0])
                    f_square(f, 1, SPEC_BANKS[1])
                    f_mag1(f)
                    if f == 0:
                        f_rs1(0)
                        f_rs2(0)
                        act.wait_ge(front_in, 16 * 7)
                        f_n1T(0)
                        f_high(0, 0)
                        f_mid(0, 0)
                        f_high(0, 1)
                        act.wait_ge(ones_made, 2)
                        f_v(0, 0)
                        f_mid(0, 1)
                maxT(0, 0)
                shift(0, 0, 0)
                f_rs1(1)
                f_rs2(1)

            def body(b, p, has_early, has_front, has_tail, has_late):
                at, f, w = PLACE, b + 1, b - 1
                for h in range(UNITS):
                    c, k = divmod(h, 8)
                    exp(b, h)
                    if k == at["act_o"]:
                        if c > 0:
                            o_copy(b, c - 1)
                        elif has_tail:
                            o_copy(w, 3)
                    if k == at["act_maxT"]:
                        if c < 3:
                            maxT(b, c + 1)
                            shift(b, p, c + 1)
                        elif has_front:
                            maxT(f, 0)
                            shift(f, 1 - p, 0)
                    if has_tail:
                        if h == at["act_attnT"]:
                            t_attnT(w)
                        if h == at["act_rstd2"]:
                            t_rs0(w)
                    if has_late:
                        if h == at["act_n3T"]:
                            t_n3T(b - 2)
                        for half in range(2):
                            if h == at["act_square3"][half]:
                                t_square(b - 2, half)
                        if h == at["act_mag3"]:
                            t_mag2(b - 2)
                    if has_front:
                        if h == at["act_n1T"]:
                            f_n1T(f)
                        if h == at["act_v"]:
                            f_v(f, 1 - p)
                        if h == at["act_high_q"]:
                            f_high(f, 0)
                        if h == at["act_mid_q"]:
                            f_mid(f, 0)
                        if h == at["act_high_k"]:
                            f_high(f, 1)
                        if h == at["act_mid_k"]:
                            f_mid(f, 1)
                    if has_tail:
                        for n in range(3):
                            if h == at["act_exp_u"][n]:
                                t_exp_u(w, n)
                            if h == at["act_ln_u"][n]:
                                t_ln_u(w, n)
                            if h == at["act_silu"][n]:
                                t_sig(w, n)
                        if h == at["act_rstd3"]:
                            t_rs1(w)
                    if has_early:
                        if h == at["act_rstd0"]:
                            f_rs0(b + 2)
                        if h == at["act_n0T"]:
                            f_n0T(b + 2)
                        for half in range(2):
                            if h == at["act_square0"][half]:
                                f_square(b + 2, half)
                        if h == at["act_mag0"]:
                            f_mag1(b + 2)
                        if h == at["act_rstd1"]:
                            f_rs1(b + 2)
                        if h == at["act_rstd1b"]:
                            f_rs2(b + 2)

            def tail():
                o_copy(last, 3)
                t_attnT(last)
                t_n3T(last - 1)
                t_rs0(last)
                t_square(last - 1, 0, SPEC_BANKS[0])
                t_square(last - 1, 1, SPEC_BANKS[1])
                for step in range(5):
                    for n, do in enumerate((t_exp_u, t_ln_u, t_sig)):
                        if 0 <= step - n < 3:
                            do(last, step - n)
                t_mag2(last - 1)
                t_rs1(last)
                t_n3T(last)
                t_square(last, 0, SPEC_BANKS[0])
                t_square(last, 1, SPEC_BANKS[1])
                t_mag2(last)

            batches(act, first, body, tail)

        @block.vector
        def _(dve):
            for i, v in enumerate((EPS, TINY, math.log(0.5), 1.0)):
                nc.vector.memset(eps_ap[:, i:i + 1], v).then_inc(consts_dve, 1)

            def angles_and_rotations():
                dve.wait_ge(angles_in, 16 * 4)
                nc.vector.tensor_tensor(ang[:, 0, :], raw[:, 0, :], raw[:, 1, :], ALU.add).then_inc(angles, 1)
                nc.vector.tensor_tensor(ang[:, 1, :], raw[:, 2, :], raw[:, 3, :], ALU.add).then_inc(angles, 1)
                dve.wait_ge(angles, 2)
                nc.vector.tensor_scalar(ang[:, 0, :], ang[:, 0, :], math.pi / 2, None, ALU.add).then_inc(angle_step, 1)
                dve.wait_ge(angle_step, 1)
                big = 1.5 * 2 ** 23
                nc.vector.tensor_scalar(turns[:], ang[:], 1 / (2 * math.pi), big, ALU.mult, ALU.add).then_inc(angle_step, 1)
                dve.wait_ge(angle_step, 2)
                nc.vector.tensor_scalar(turns[:], turns[:], big, None, ALU.subtract).then_inc(angle_step, 1)
                dve.wait_ge(angle_step, 3)
                nc.vector.scalar_tensor_tensor(out=ang[:], in0=turns[:], scalar=-6.28125, in1=ang[:],
                                               op0=ALU.mult, op1=ALU.add).then_inc(angle_step, 1)
                dve.wait_ge(angle_step, 4)
                nc.vector.scalar_tensor_tensor(out=ang[:], in0=turns[:], scalar=-(2 * math.pi - 6.28125), in1=ang[:],
                                               op0=ALU.mult, op1=ALU.add).then_inc(angle_step, 1)
                dve.wait_ge(angle_step, 5)
                nc.vector.tensor_scalar(ang[:], ang[:], float(np.float32(3.1415925)), -float(np.float32(3.1415925)),
                                        ALU.min, ALU.max).then_inc(angles, 4)
                dve.wait_ge(qk_in, 16 * 2)
                for i in (0, 2):
                    src = wqk[:, i, :].rearrange("p (j e) -> p j e", e=2)
                    dst = wqk[:, i + 1, :].rearrange("p (j e) -> p j e", e=2)
                    nc.vector.tensor_scalar(dst[:, :, 0], src[:, :, 1], -1.0, None, ALU.mult).then_inc(rot_ready, 1)
                    nc.vector.tensor_copy(dst[:, :, 1], src[:, :, 0]).then_inc(rot_ready, 1)

            def stats(src, st, s_st):
                for t in range(TILES):
                    ins = nc.vector.bn_stats(st[:, t, :], src[:, t, :])
                ins.then_inc(s_st, 1)

            def moments(st, mv, negm, s_st, s_mv, s_neg, n):
                wait_alone(dve, s_st, n)
                for t in range(TILES):
                    ins = nc.vector.bn_aggr(mv[:, t, :], st[:, t, :])
                ins.then_inc(s_mv, 1)
                dve.wait_ge(s_mv, n)
                nc.vector.tensor_scalar(negm, mv[:, :, 0], -1.0, None, ALU.mult).then_inc(s_neg, 1)

            def norm(dst, src, negm, rs, negm_sem, rs_sem, done, n):
                dve.wait_ge(rs_sem, n)
                wait_alone(dve, negm_sem, n)
                for t in range(TILES):
                    ins = nc.vector.tensor_scalar(dst[:, t, :], src[:, t, :], negm[:, t:t + 1], rs[:, t:t + 1],
                                                  ALU.add, ALU.mult)
                ins.then_inc(done, 1)

            def f_stats0(f, p):
                dve.wait_ge(x_in, 16 * (f + 1))
                stats(xt[:, p], f_st[:, 0], x_stats)

            def f_moments0(f):
                moments(f_st[:, 0], f_mv[:, 0], f_negm[:, 0, :], x_stats, x_mv, x_negm, f + 1)

            def f_z1(f):
                dve.wait_ge(early_act, 3 * f + 3)
                nc.vector.tensor_tensor(f_z[:, :, :], f_sq[:, :, 0:P], f_sq[:, :, P:2 * P], ALU.add).then_inc(z1_ready, 1)

            def f_x1(f, p):
                dve.wait_ge(mag1, f + 1)
                if not (isinstance(f, int) and f < 1):
                    wait_alone(dve, xy_ready, f)
                nc.vector.tensor_tensor(x1[:, :, :], xt[:, p, :, :], f_z[:, :, :], ALU.add).then_inc(x1_ready, 1)

            def f_stats1(f):
                dve.wait_ge(x1_ready, f + 1)
                stats(x1, f_st[:, 1], x1_stats)

            def f_moments1(f):
                moments(f_st[:, 1], f_mv[:, 1], f_negm[:, 1, :], x1_stats, x1_mv, x1_negm, f + 1)

            def f_vy(f):
                dve.wait_ge(x1_rstd, f + 1)
                nc.vector.tensor_tensor(f_vyt[:, 0, :], f_mv[:, 1, :, 1], f_rs[:, 1, :], ALU.mult).then_inc(vy_part, 1)
                dve.wait_ge(vy_part, f + 1)
                nc.vector.tensor_tensor(f_vyt[:, 1, :], f_vyt[:, 0, :], f_rs[:, 1, :], ALU.mult).then_inc(vy_ready, 1)

            def f_rs2(f):
                dve.wait_ge(vy_rstd, f + 1)
                nc.vector.tensor_tensor(f_rs[:, 3, :], f_rs[:, 1, :], f_rs[:, 2, :], ALU.mult).then_inc(rs2_ready, 1)

            def f_rot(f, i, j, bank=None):
                dve.wait_ge(front_mm, 6 * f + 2 + 2 * i + j)
                nc.vector.tensor_tensor(rot[:, i, j, :], f_ps[:, :] if bank is None else bank, (sin_sb if j else cos_sb)[:, :], ALU.mult).then_inc(front_read, 1)

            def f_resid_k(f):
                dve.wait_ge(high_ready, 2 * f + 2)
                nc.vector.tensor_tensor(resid[:, 1, :], roped[:, 1, :], parts[:, 1, 0, :], ALU.subtract).then_inc(resid_k, 1)

            def f_low_k(f):
                dve.wait_ge(mid_ready, 2 * f + 2)
                nc.vector.tensor_tensor(parts[:, 1, 2, :], resid[:, 1, :], parts[:, 1, 1, :], ALU.subtract).then_inc(low_k, 1)

            def amax(a, c, j):
                dve.wait_ge(max_scores, A_USES * (4 * a + c) + j + 1)
                bank = a_ps[:, j % 2, :]
                if j == 0:
                    dst = mx[:, c % 2, :, :, 0]
                    src = bank.rearrange("p (s g n) -> p s g n", s=2, g=2)
                else:
                    t, pr = (j + 1) // 2, (j + 1) % 2
                    dst, src = mx[:, c % 2, pr, :, t], bank.rearrange("p (g n) -> p g n", g=2)
                nc.vector.tensor_reduce(dst, src, AX, ALU.max).then_inc(max_done, 1)

            def o_norm(b, c):
                dve.wait_ge(oT_mm, 4 * b + c + 1)
                oT = o_ps[:, :].rearrange("p (t h n) -> p t h n", t=TILES, h=4)
                nc.vector.reciprocal(rden[:, :, :], oT[:, :, :, HD]).then_inc(den_done, 1)
                dve.wait_ge(den_done, 4 * b + c + 1)
                if c == 0 and not (isinstance(b, int) and b < 1):
                    dve.wait_ge(tail_mm, 10 * (b - 1) + 1)
                for t in range(TILES):
                    dst = attn[:, t, 32 * c:32 * c + 32].rearrange("p (h d) -> p h d", h=4)
                    ins = nc.vector.tensor_tensor(dst, oT[:, t, :, 0:HD],
                                                  rden[:, t, :].unsqueeze(2).to_broadcast([P, 4, HD]), ALU.mult)
                ins.then_inc(attn_done, 1)

            def t_h(w, p):
                wait_alone(dve, xy_ready, w + 1)
                dve.wait_ge(tail_mm, 10 * w + 2)
                nc.vector.tensor_tensor(h[:, :, :], t_ps[:, :].rearrange("p (t n) -> p t n", t=TILES),
                                        y[:, p, :, :], ALU.add)
                nc.vector.tensor_tensor(hx1[:, :, :], t_ps[:, :].rearrange("p (t n) -> p t n", t=TILES),
                                        xy[:, p, :, :], ALU.add).then_inc(tail_read, 1)

            def t_stats2(w):
                dve.wait_ge(tail_read, 10 * w + 2)
                stats(h, t_st[:, 0], h_stats)

            def t_moments2(w):
                moments(t_st[:, 0], t_mv[:, 0], t_negm[:, 0, :], h_stats, h_mv, h_negm, w + 1)

            def t_n2T(w):
                dve.wait_ge(tail_mm, 10 * w + 3)
                nc.vector.tensor_scalar(n2T[:, :], t_ps[:, :], gb[:, 2:3], gb[:, 3:4], ALU.mult, ALU.add).then_inc(tail_read, 1)

            def t_up(w, c, banks):
                r = CHUNKS[c][1]
                dve.wait_ge(tail_mm, 10 * w + 4 + c)
                nc.vector.tensor_scalar(up[0:r, c, :], banks[c][0:r, :], -43.0, None, ALU.max).then_inc(tail_read, 1)

            def t_gate(w, c, banks):
                r = CHUNKS[c][1]
                dve.wait_ge(tail_mm, 10 * w + 7 + c)
                dve.wait_ge(silu_u, 3 * w + c + 1)
                nc.vector.tensor_tensor(gated[0:r, c, :], banks[3 + c][0:r, :], act_up[0:r, c, :], ALU.mult).then_inc(tail_read, 1)

            def t_x2(w):
                dve.wait_ge(tail_mm, 10 * w + 10)
                if not (isinstance(w, int) and w < 1):
                    dve.wait_ge(x3_ready, w)
                nc.vector.tensor_tensor(x2[:, :, :], t_ps[:, :].rearrange("p (t n) -> p t n", t=TILES),
                                        hx1[:, :, :], ALU.add).then_inc(tail_read, 1)

            def t_stats3(w):
                dve.wait_ge(tail_read, 10 * w + 10)
                stats(x2, t_st[:, 1], x2_stats)

            def t_moments3(w):
                moments(t_st[:, 1], t_mv[:, 1], t_negm[:, 1, :], x2_stats, x2_mv, x2_negm, w + 1)

            def t_z2(w):
                dve.wait_ge(late_act, 3 * w + 3)
                nc.vector.tensor_tensor(t_z[:, :, :], t_sq[:, :, 0:P], t_sq[:, :, P:2 * P], ALU.add).then_inc(z2_ready, 1)

            def t_x3(w):
                dve.wait_ge(mag2, w + 1)
                dve.wait_ge(stored, 16 * w + 16)
                nc.vector.tensor_tensor(x3[:, :, :], x2[:, :, :], t_z[:, :, :], ALU.add).then_inc(x3_ready, 1)

            def first():
                f_stats0(0, 0)
                f_moments0(0)
                angles_and_rotations()
                norm(n0, xt[:, 0], f_negm[:, 0], f_rs[:, 0], x_negm, x_rstd, n0_ready, 1)
                nc.vector.memset(qz[:], 0.0).then_inc(consts_dve, 1)
                f_z1(0)
                f_x1(0, 0)
                f_stats1(0)
                f_moments1(0)
                f_vy(0)
                f_rs2(0)
                norm(yn, x1, f_negm[:, 1], f_rs[:, 3], x1_negm, rs2_ready, yn_ready, 1)
                dve.wait_ge(front_in, 16 * 7)
                for i in range(4):
                    f_rot(0, i // 2, i % 2, FIRST_BANKS[i])
                f_resid_k(0)
                f_low_k(0)
                f_stats0(1, 1)
                f_moments0(1)
                f_z1(1)
                for j in range(A_USES):
                    amax(0, 0, j)
                f_x1(1, 1)
                f_stats1(1)
                f_moments1(1)
                f_vy(1)
                f_rs2(1)

            def body(b, p, has_early, has_front, has_tail, has_late):
                at, f, w = PLACE, b + 1, b - 1
                for h in range(UNITS):
                    c, k = divmod(h, 8)
                    uses = MAX_AT[k] if c < 3 or has_front else ()
                    a = (b, c + 1) if c < 3 else (f, 0)
                    for j in uses[0:1]:
                        amax(*a, j)
                    if k == at["dve_o"]:
                        if c > 0:
                            o_norm(b, c - 1)
                        elif has_tail:
                            o_norm(w, 3)
                    if has_late:
                        if h == at["dve_z3"]:
                            t_z2(b - 2)
                        if h == at["dve_x3"]:
                            t_x3(b - 2)
                    if has_tail:
                        if h == at["dve_h"]:
                            t_h(w, 1 - p)
                        if h == at["dve_stats2"]:
                            t_stats2(w)
                        if h == at["dve_moments2"]:
                            t_moments2(w)
                        if h == at["dve_n2T"]:
                            t_n2T(w)
                        for n in range(3):
                            if h == at["dve_up"][n]:
                                t_up(w, n, FFN_BANKS)
                        for n in range(3):
                            if h == at["dve_gate"][n]:
                                t_gate(w, n, FFN_BANKS)
                        if h == at["dve_x2"]:
                            t_x2(w)
                        if h == at["dve_stats3"]:
                            t_stats3(w)
                        if h == at["dve_moments3"]:
                            t_moments3(w)
                    for j in uses[1:]:
                        amax(*a, j)
                    if has_front:
                        for i in range(4):
                            if h == at["dve_rot"][i]:
                                f_rot(f, i // 2, i % 2)
                        if h == at["dve_resid_k"]:
                            f_resid_k(f)
                        if h == at["dve_low_k"]:
                            f_low_k(f)
                    if has_early:
                        if h == at["dve_stats0"]:
                            f_stats0(b + 2, p)
                        if h == at["dve_moments0"]:
                            f_moments0(b + 2)
                        if h == at["dve_z0"]:
                            f_z1(b + 2)
                        if h == at["dve_x1"]:
                            f_x1(b + 2, p)
                        if h == at["dve_stats1"]:
                            f_stats1(b + 2)
                        if h == at["dve_moments1"]:
                            f_moments1(b + 2)
                        if h == at["dve_rstd1"]:
                            f_vy(b + 2)
                            f_rs2(b + 2)

            def tail():
                o_norm(last, 3)
                t_h(last, last % 2)
                t_stats2(last)
                t_moments2(last)
                norm(n2, h, t_negm[:, 0], t_rs[:, 0], h_negm, h_rstd, n2_ready, last + 1)
                t_n2T(last)
                for c in range(3):
                    t_up(last, c, LAST_BANKS)
                t_z2(last - 1)
                for c in range(3):
                    t_gate(last, c, LAST_BANKS)
                t_x3(last - 1)
                t_x2(last)
                t_stats3(last)
                t_moments3(last)
                norm(n3, x2, t_negm[:, 1], t_rs[:, 1], x2_negm, x2_rstd, n3_ready, last + 1)
                t_z2(last)
                t_x3(last)

            batches(dve, first, body, tail)

        @block.tensor
        def _(pe):
            mm = nc.tensor.matmul
            pe.wait_ge(masks_made, 4)

            def transposes(dst, src, done):
                for t in range(TILES):
                    ins = nc.tensor.transpose(dst[:, t * P:(t + 1) * P], src[:, t, :], ident[:, :])
                ins.then_inc(done, 1)

            def spectral(dst, srcT, half, done):
                for i in range(2):
                    t = 2 * half + i
                    ins = mm(dst[:, i * 2 * P:(i + 1) * 2 * P], srcT[:, t * P:(t + 1) * P], spec_w[:, :],
                             start=True, stop=True)
                ins.then_inc(done, 1)

            def f_T0(f):
                pe.wait_ge(n0_ready, f + 1)
                if not (isinstance(f, int) and f < 1):
                    pe.wait_ge(front_read, 6 * f)
                transposes(f_ps, n0, early_mm)

            def f_spec(f, half, bank=None):
                pe.wait_ge(early_act, 3 * f + 1 + (half if bank is None else 0))
                spectral(f_ps if bank is None else bank, n0T, half, early_mm)

            def f_T1(f):
                pe.wait_ge(yn_ready, f + 1)
                pe.wait_ge(early_act, 3 * f + 3)
                transposes(f_ps, yn, front_mm)

            def f_proj(f, i, bank=None):
                pe.wait_ge(front_read, 6 * f + 1 + (i if bank is None else 0))
                mm(f_ps[:, :] if bank is None else bank, wqk[:, i, :], n1T[:, :], start=True, stop=True).then_inc(front_mm, 1)

            def f_v(f):
                pe.wait_ge(front_read, 6 * f + 5)
                for t in range(TILES):
                    ins = mm(f_ps[:, t * P:(t + 1) * P], n1T[:, t * P:(t + 1) * P], wv_sb[:, :], start=True, stop=True)
                ins.then_inc(front_mm, 1)

            def amax(a, p, c, j):
                quad = 4 * a + c
                if c == 0 and j == 0:
                    pe.wait_ge(k_stacked, K_DMAS * (a + 1))
                    pe.wait_ge(q_stacked, Q_DMAS * (a + 1))
                first_ever = isinstance(a, int) and a == 0 and c == 0
                if j >= 2 or (j == 0 and not first_ever):
                    pe.wait_ge(max_done, A_USES * quad + max(j - 1, 0))
                if j == 1 and not first_ever:
                    pe.wait_ge(maxT_out, quad)
                bank = a_ps[:, j % 2, :]
                if j == 0:
                    mm(bank, ident_b[:, :], causal_mask[:].rearrange("p h n -> p (h n)"), start=True, stop=True)
                    for hh in range(4):
                        pr, g = 2 * c + hh // 2, hh % 2
                        ins = mm(bank[:, hh * P:(hh + 1) * P], qz[0:SPLIT_ROWS, p, pr, g, 0:P],
                                 ks[0:SPLIT_ROWS, p, pr, 0:P], start=False, stop=True, skip_group_check=True)
                else:
                    t, pr = (j + 1) // 2, 2 * c + (j + 1) % 2
                    mm(bank, ident_b[:, :], band_mask[:].rearrange("p h n -> p (h n)"), start=True, stop=True)
                    for g in range(2):
                        ins = mm(bank[:, g * 2 * P:(g + 1) * 2 * P], qz[0:SPLIT_ROWS, p, pr, g, t * P:(t + 1) * P],
                                 ks[0:SPLIT_ROWS, p, pr, (t - 1) * P:(t + 1) * P], start=False, stop=True,
                                 skip_group_check=True)
                ins.then_inc(max_scores, 1)

            def maxT(a, c):
                pe.wait_ge(max_done, A_USES * (4 * a + c + 1))
                nc.tensor.transpose(a_ps[0:16, 1, 0:P], mx[:, c % 2, :, :, :].rearrange("p s g t -> p (s g t)"),
                                    ident[:, :]).then_inc(maxT_mm, 1)

            def score(b, p, v):
                c, kt, pr = v // 8, (v % 8) // 2, 2 * (v // 8) + v % 2
                if v % 8 == 0:
                    pe.wait_ge(shift_in, 16 * (4 * b + c + 1))
                if not (isinstance(b, int) and 32 * b + v < 3):
                    pe.wait_ge(exp_done, 32 * b + (v - 2 if v > 1 else v - 1))
                n = 2 * P if kt < 3 else P
                mm(s_ps[:, v % 3, 0:2 * n], ks[0:SHIFT_ROWS, p, pr, kt * P:(kt + 1) * P],
                   qz[0:SHIFT_ROWS, p, pr, :, kt * P:kt * P + n], start=True, stop=True).then_inc(scores, 1)

            def pv(b, p, s):
                c, kt = divmod(s, 4)
                pe.wait_ge(masked, 16 * b + s + 1)
                if kt == 0 and not (isinstance(b, int) and 4 * b + c < 1):
                    pe.wait_ge(attn_done, 4 * b + c)
                n = 2 * P if kt < 3 else P
                for hh in range(4):
                    ins = mm(o_ps[32 * hh:32 * hh + 32, kt * P:kt * P + n], vaug[:, p, kt, 4 * c + hh, :],
                             prob[:, s % 4, hh // 2, hh % 2, 0:n], start=(kt == 0), stop=(kt == 3),
                             skip_group_check=True)
                ins.then_inc(pv_done, 1)

            def oT(b, c):
                pe.wait_ge(o_out, 4 * b + c + 1)
                for t in range(TILES):
                    ins = nc.tensor.transpose(o_ps[:, t * P:(t + 1) * P], o_sb[:, t * P:(t + 1) * P], ident[:, :])
                ins.then_inc(oT_mm, 1)

            def t_attn(w):
                pe.wait_ge(attn_done, 4 * w + 4)
                if not (isinstance(w, int) and w < 1):
                    pe.wait_ge(tail_read, 10 * w)
                transposes(t_ps, attn, tail_mm)

            def t_wo(w):
                pe.wait_ge(tail_read, 10 * w + 1)
                for t in range(TILES):
                    ins = mm(t_ps[:, t * P:(t + 1) * P], attnT[:, t * P:(t + 1) * P], wo_sb[:, :], start=True, stop=True)
                ins.then_inc(tail_mm, 1)

            def t_n2(w):
                pe.wait_ge(n2_ready, w + 1)
                if isinstance(w, int) and w < 1:
                    pe.wait_ge(tail_read, 2)
                else:
                    pe.wait_ge(late_act, 3 * w)
                transposes(t_ps, n2, tail_mm)

            def t_ffn(w, i, fronts=None):
                at, r = CHUNKS[i % 3]
                if fronts is None or i == 0:
                    pe.wait_ge(tail_read, 10 * w + 3)
                elif i == 1:
                    pe.wait_ge(front_read, 6 * fronts)
                else:
                    pe.wait_ge(tail_read, 10 * w + 2 + i)
                bank = (LAST_BANKS if fronts is None else FFN_BANKS)[i]
                mm(bank[0:r, :], (w3_sb if i >= 3 else w1_sb)[:, at:at + r], n2T[:, :],
                   start=True, stop=True).then_inc(tail_mm, 1)

            def t_w2(w, c):
                pe.wait_ge(tail_read, 10 * w + max(7 + c, 8))
                r = CHUNKS[c][1]
                for t in range(TILES):
                    ins = mm(t_ps[:, t * P:(t + 1) * P], gated[0:r, c, t * P:(t + 1) * P], w2_sb[0:r, c, :],
                             start=(c == 0 and t == 0), stop=(c == 2), skip_group_check=True)
                if c == 2:
                    ins.then_inc(tail_mm, 1)

            def t_n3(w):
                pe.wait_ge(n3_ready, w + 1)
                if isinstance(w, int) and w >= last - 1:
                    pe.wait_ge(tail_read, 10 * last + (10 if w == last else 2))
                else:
                    pe.wait_ge(tail_read, 10 * w + 12)
                transposes(t_ps, n3, late_mm)

            def t_spec(w, half, bank=None):
                pe.wait_ge(late_act, 3 * w + 1 + (half if bank is None else 0))
                spectral(t_ps if bank is None else bank, n3T, half, late_mm)

            def first():
                for f in range(2):
                    f_T0(f)
                    if f == 0:
                        pe.wait_ge(spec_ready, 2)
                    f_spec(f, 0, SPEC_BANKS[0])
                    f_spec(f, 1, SPEC_BANKS[1])
                    if f == 0:
                        f_T1(0)
                        pe.wait_ge(rot_ready, 4)
                        for i in range(4):
                            f_proj(0, i, FIRST_BANKS[i])
                        f_v(0)
                pe.wait_ge(early_act, 6)
                for j in range(A_USES):
                    amax(0, 0, 0, j)
                maxT(0, 0)
                pe.wait_ge(ones_made, 2)
                pe.wait_ge(tail_in, 16 * 5)

            def body(b, p, has_early, has_front, has_tail, has_late):
                at, f, w = PLACE, b + 1, b - 1
                fronts = b + 2 if has_front else BATCH
                for h in range(UNITS):
                    c, k = divmod(h, 8)
                    uses = MAX_AT[k] if c < 3 or has_front else ()
                    a = (b, p, c + 1) if c < 3 else (f, 1 - p, 0)
                    score(b, p, h)
                    if h == 1 and has_tail:
                        pv(w, 1 - p, 15)
                    for j in uses[0:1]:
                        amax(*a, j)
                    if k == at["pe_oT"]:
                        if c > 0:
                            oT(b, c - 1)
                        elif has_tail:
                            oT(w, 3)
                    if has_tail:
                        if h == at["pe_T2"]:
                            t_n2(w)
                        for n in range(3):
                            if h == at["pe_up"][n]:
                                t_ffn(w, n, fronts)
                        for n in range(3):
                            if h == at["pe_gate"][n]:
                                t_ffn(w, 3 + n, fronts)
                        for n in range(3):
                            if h == at["pe_w2"][n]:
                                t_w2(w, n)
                    if has_late:
                        if h == at["pe_T3"]:
                            t_n3(b - 2)
                        for half in range(2):
                            if h == at["pe_spec3"][half]:
                                t_spec(b - 2, half)
                    for j in uses[1:]:
                        amax(*a, j)
                    if has_tail:
                        if h == at["pe_attn"]:
                            t_attn(w)
                        if h == at["pe_wo"]:
                            t_wo(w)
                    if has_front:
                        if h == at["pe_T1"]:
                            f_T1(f)
                        for i in range(4):
                            if h == at["pe_proj"][i]:
                                f_proj(f, i)
                        if h == at["pe_v"]:
                            f_v(f)
                    if has_early:
                        if h == at["pe_T0"]:
                            if has_tail:
                                pe.wait_ge(tail_read, 10 * w + 9)
                            f_T0(b + 2)
                        for half in range(2):
                            if h == at["pe_spec0"][half]:
                                f_spec(b + 2, half)
                    if k == at["pe_maxT"] and (c < 3 or has_front):
                        maxT(a[0], a[2])
                    if h % 2 == 1 and h >= 5:
                        s = (h - 3) // 2
                        if s % 4 == 1:
                            pv(b, p, s - 1)
                        if s % 4 != 0:
                            pv(b, p, s)

            def tail():
                w, p = last, last % 2
                pv(w, p, 15)
                oT(w, 3)
                t_attn(w)
                t_wo(w)
                t_n3(w - 1)
                t_spec(w - 1, 0, SPEC_BANKS[0])
                t_spec(w - 1, 1, SPEC_BANKS[1])
                t_n2(w)
                for i in range(6):
                    t_ffn(w, i)
                for c in range(3):
                    t_w2(w, c)
                t_n3(w)
                t_spec(w, 0, SPEC_BANKS[0])
                t_spec(w, 1, SPEC_BANKS[1])

            batches(pe, first, body, tail)


_INS = ['L0_attn_x', 'L0_attn_wq', 'L0_attn_wk', 'L0_attn_wv', 'L0_attn_wo', 'L0_attn_w1', 'L0_attn_w2', 'L0_attn_w3',
        'L0_attn_ln1_g', 'L0_attn_ln1_b', 'L0_attn_ln2_g', 'L0_attn_ln2_b', 'L0_ffn_theta', 'L0_ffn_phi',
        'L0_ffn_theta_noise', 'L0_ffn_phi_noise']


def rope_tables():
    freqs = (1.0 / np.float32(THETA) ** (np.arange(0, HD, 2, dtype=np.float32) / np.float32(HD))).astype(np.float32)
    angle = np.outer(freqs, np.arange(SEQ, dtype=np.float32)).astype(np.float32)
    rows = np.tile(np.repeat(angle, 2, axis=0), (HEADS, 1))
    return np.cos(rows).astype(np.float32), np.sin(rows).astype(np.float32)


def kernel(**inputs):
    import concourse.bacc as bacc
    from concourse.bass_utils import run_bass_kernel_spmd as run

    nc = bacc.Bacc("TRN2", target_bir_lowering=False, num_devices=1)
    arrays, aps = {}, {}

    def give(name, a):
        arrays[name] = a
        aps[name] = nc.dram_tensor(name, a.shape, mybir.dt.from_np(a.dtype), kind="ExternalInput").ap()

    for name in _INS:
        a = np.ascontiguousarray(inputs[name])
        give(name, a.reshape(DIM, 1) if a.ndim == 1 else a)
    cos_t, sin_t = rope_tables()
    give("cos_table", cos_t)
    give("sin_table", sin_t)
    out = nc.dram_tensor("out", (BATCH, SEQ, DIM), FP32, kind="ExternalOutput").ap()
    a = {n.replace("L0_attn_", "").replace("L0_ffn_", ""): v for n, v in aps.items()}
    build(nc, a["x"], a["cos_table"], a["sin_table"], a["wq"], a["wk"], a["wv"], a["wo"], a["w1"], a["w2"], a["w3"],
          a["ln1_g"], a["ln1_b"], a["ln2_g"], a["ln2_b"], a["theta"], a["phi"], a["theta_noise"], a["phi_noise"], out)
    r = run(nc, [arrays], core_ids=[0])
    return r.results[0]["out"]
```
